# Optimizing a Trainium2 kernel written in Bass

```python
import numpy as np
import jax
import jax.numpy as jnp

def _softmax(x, axis=-1):
    return jax.nn.softmax(x, axis=axis)

def _gelu(x):
    return jax.nn.gelu(x, approximate=True)

def _silu(x):
    return jax.nn.silu(x)

def _sigmoid(x):
    return jax.nn.sigmoid(x)

def _layernorm(x, axis=-1, eps=1e-05):
    m = jnp.mean(x, axis=axis, keepdims=True)
    v = jnp.var(x, axis=axis, keepdims=True)
    return (x - m) / jnp.sqrt(v + eps)

def _scatter_add(tgt, idx, src, axis=0):
    return tgt.at[idx].add(src)

def _segment_sum(src, seg, n):
    return jax.ops.segment_sum(src, seg, n)
kernel_name = 'mk_seq_preln_d1_jaxref_r4_6f2c23'

def setup_inputs(seed: int=0):
    np.random.seed(seed)
    _w = jnp.asarray

    def _L0_attn_setup():
        import jax, jax.numpy as jnp
        import numpy as np
        B, T, D = (2, 512, 256)
        H = 16
        DH = D // H
        EPS = 1e-06

        def _feature_map(x):
            return jax.nn.elu(x) + 1.0
        key = jax.random.key(seed)
        ks = jax.random.split(key, 9)
        s = 0.02
        return {'x': jax.random.normal(ks[0], (B, T, D), dtype=jnp.float32), 'Wq': jax.random.normal(ks[1], (D, D), dtype=jnp.float32) * s, 'bq': jnp.zeros((D,), dtype=jnp.float32), 'Wk': jax.random.normal(ks[2], (D, D), dtype=jnp.float32) * s, 'bk': jnp.zeros((D,), dtype=jnp.float32), 'Wv': jax.random.normal(ks[3], (D, D), dtype=jnp.float32) * s, 'bv': jnp.zeros((D,), dtype=jnp.float32), 'Wo': jax.random.normal(ks[4], (D, D), dtype=jnp.float32) * s, 'bo': jnp.zeros((D,), dtype=jnp.float32)}
    _L0_attn_in = _L0_attn_setup()

    def _L0_ffn_setup():
        import jax, jax.numpy as jnp
        import numpy as np
        D_MODEL = 256
        HIDDEN = 256
        NUM_EXPERTS = 8
        TOP_K = 2
        key = jax.random.key(seed)
        ks = jax.random.split(key, 10)
        s = 0.02
        return {'x': jax.random.normal(ks[0], (2, 512, D_MODEL), dtype=jnp.float32), 'gate_w': jax.random.normal(ks[1], (NUM_EXPERTS, D_MODEL), dtype=jnp.float32) * s, 'up_w': jax.random.normal(ks[2], (NUM_EXPERTS, D_MODEL, HIDDEN), dtype=jnp.float32) * s, 'up_b': jnp.zeros((NUM_EXPERTS, HIDDEN), dtype=jnp.float32), 'down_w': jax.random.normal(ks[3], (NUM_EXPERTS, HIDDEN, D_MODEL), dtype=jnp.float32) * s, 'down_b': jnp.zeros((NUM_EXPERTS, D_MODEL), dtype=jnp.float32), 'sh_up_w': jax.random.normal(ks[4], (D_MODEL, HIDDEN), dtype=jnp.float32) * s, 'sh_up_b': jnp.zeros((HIDDEN,), dtype=jnp.float32), 'sh_down_w': jax.random.normal(ks[5], (HIDDEN, D_MODEL), dtype=jnp.float32) * s, 'sh_down_b': jnp.zeros((D_MODEL,), dtype=jnp.float32)}
    _L0_ffn_in = _L0_ffn_setup()
    _d = {'L0_attn_x': _L0_attn_in['x'], 'L0_attn_Wq': _L0_attn_in['Wq'], 'L0_attn_bq': _L0_attn_in['bq'], 'L0_attn_Wk': _L0_attn_in['Wk'], 'L0_attn_bk': _L0_attn_in['bk'], 'L0_attn_Wv': _L0_attn_in['Wv'], 'L0_attn_bv': _L0_attn_in['bv'], 'L0_attn_Wo': _L0_attn_in['Wo'], 'L0_attn_bo': _L0_attn_in['bo'], 'L0_ffn_gate_w': _L0_ffn_in['gate_w'], 'L0_ffn_up_w': _L0_ffn_in['up_w'], 'L0_ffn_up_b': _L0_ffn_in['up_b'], 'L0_ffn_down_w': _L0_ffn_in['down_w'], 'L0_ffn_down_b': _L0_ffn_in['down_b'], 'L0_ffn_sh_up_w': _L0_ffn_in['sh_up_w'], 'L0_ffn_sh_up_b': _L0_ffn_in['sh_up_b'], 'L0_ffn_sh_down_w': _L0_ffn_in['sh_down_w'], 'L0_ffn_sh_down_b': _L0_ffn_in['sh_down_b']}
    _x0 = _d['L0_attn_x']
    _d['L0_attn_x'] = jax.random.normal(jax.random.fold_in(jax.random.key(seed), 1), (2, 2048, 256), dtype=_x0.dtype)
    del _x0
    return _d

def reference(L0_attn_x, L0_attn_Wq, L0_attn_bq, L0_attn_Wk, L0_attn_bk, L0_attn_Wv, L0_attn_bv, L0_attn_Wo, L0_attn_bo, L0_ffn_gate_w, L0_ffn_up_w, L0_ffn_up_b, L0_ffn_down_w, L0_ffn_down_b, L0_ffn_sh_up_w, L0_ffn_sh_up_b, L0_ffn_sh_down_w, L0_ffn_sh_down_b):

    def _L0_attn_ref(x, Wq, bq, Wk, bk, Wv, bv, Wo, bo):
        import jax, jax.numpy as jnp
        import numpy as np
        B, T, D = (2, 512, 256)
        H = 16
        DH = D // H
        EPS = 1e-06

        def _feature_map(x):
            return jax.nn.elu(x) + 1.0
        b, t, d = x.shape
        q = (x @ Wq.T + bq).reshape(b, t, H, DH).transpose(0, 2, 1, 3)
        k = (x @ Wk.T + bk).reshape(b, t, H, DH).transpose(0, 2, 1, 3)
        v = (x @ Wv.T + bv).reshape(b, t, H, DH).transpose(0, 2, 1, 3)
        q = _feature_map(q)
        k = _feature_map(k)
        kv = jnp.einsum('bhtd,bhte->bhtde', k, v)
        kv_cum = jnp.cumsum(kv, axis=2)
        numerator = jnp.einsum('bhtd,bhtde->bhte', q, kv_cum)
        k_cum = jnp.cumsum(k, axis=2)
        denominator = jnp.einsum('bhtd,bhtd->bht', q, k_cum)
        denominator = jnp.maximum(denominator, EPS)[..., None]
        out = numerator / denominator
        out = out.transpose(0, 2, 1, 3).reshape(b, t, d)
        return out @ Wo.T + bo

    def _L0_ffn_ref(x, gate_w, up_w, up_b, down_w, down_b, sh_up_w, sh_up_b, sh_down_w, sh_down_b):
        import jax, jax.numpy as jnp
        import numpy as np
        D_MODEL = 256
        HIDDEN = 256
        NUM_EXPERTS = 8
        TOP_K = 2
        b, s, d = x.shape
        xf = x.reshape(-1, d)
        shared = jax.nn.silu(x @ sh_up_w + sh_up_b) @ sh_down_w + sh_down_b
        logits = xf @ gate_w.T
        scores = jax.nn.softmax(logits, axis=-1)
        topk_w, topk_i = jax.lax.top_k(scores, TOP_K)
        topk_w = topk_w / (topk_w.sum(axis=-1, keepdims=True) + 1e-20)
        comb = (jax.nn.one_hot(topk_i, NUM_EXPERTS, dtype=xf.dtype) * topk_w[..., None]).sum(axis=1)
        h = jnp.einsum('nd,edh->neh', xf, up_w) + up_b
        h = jax.nn.silu(h)
        ye = jnp.einsum('neh,ehd->ned', h, down_w) + down_b
        y = jnp.einsum('ned,ne->nd', ye, comb).reshape(b, s, d)
        return y + shared
    x = L0_attn_x
    x = x + _L0_attn_ref(_layernorm(x, axis=-1), L0_attn_Wq, L0_attn_bq, L0_attn_Wk, L0_attn_bk, L0_attn_Wv, L0_attn_bv, L0_attn_Wo, L0_attn_bo)
    x = x + _L0_ffn_ref(_layernorm(x, axis=-1), L0_ffn_gate_w, L0_ffn_up_w, L0_ffn_up_b, L0_ffn_down_w, L0_ffn_down_b, L0_ffn_sh_up_w, L0_ffn_sh_up_b, L0_ffn_sh_down_w, L0_ffn_sh_down_b)
    return x

_drawn_inputs = setup_inputs


def setup_inputs(seed=0):
    import zlib

    import numpy as np

    out = dict(_drawn_inputs(seed))
    spreads = {'L0_attn_bq': (0.0, 2.0),
     'L0_attn_bk': (0.0, 2.0),
     'L0_attn_bv': (0.0, 0.1),
     'L0_attn_bo': (0.0, 0.1),
     'L0_ffn_up_b': (0.0, 0.683),
     'L0_ffn_down_b': (0.0, 0.1),
     'L0_ffn_sh_up_b': (0.0, 0.475),
     'L0_ffn_sh_down_b': (0.0, 0.1)}
    factors = {'L0_attn_Wq': 22.239, 'L0_attn_Wk': 8.0, 'L0_attn_Wv': 7.22}
    for name, (base, spread) in spreads.items():
        noise = np.random.default_rng([zlib.crc32(name.encode()), seed]).standard_normal(out[name].shape)
        drawn = base * np.exp(spread * noise) if base else spread * noise
        out[name] = jnp.asarray(drawn.astype(out[name].dtype))
    for name, factor in factors.items():
        out[name] = (out[name] * factor).astype(out[name].dtype)
    return out
```

```python
from contextlib import ExitStack

import concourse.bass as bass
from concourse import mybir

P = 128
ALU = mybir.AluOpType
ACT = mybir.ActivationFunctionType
AX_X = mybir.AxisListType.X
F32 = mybir.dt.float32
F32R = mybir.dt.float32r

B, T, D = 2, 2048, 256
H, DH = 16, 16
NE = 8
HID = 256
TOK = 512
CH = TOK // P
NT = B * T // TOK
TPB = T // TOK
KC = D // P
HG = 4
NG = H // HG
HH = H // KC
SLOT = 32
VW = DH + 1
EPS_LN = 1e-5
EPS_DEN = 1e-6
GAPS = 20

GAP_OF = {("LN1", k): 0 for k in range(KC)}
GAP_OF.update({("Q", k): 1 for k in range(KC)})
GAP_OF.update({("K", k): 1 for k in range(KC)})
GAP_OF.update({("V", k): 2 for k in range(CH // 2)})
GAP_OF.update({("KT", k): 3 for k in range(CH // 2)})
CORE = 5


def gap_products():
    gaps = [[] for _ in range(GAPS)]
    for (name, k), g in GAP_OF.items():
        gaps[g].append((name, k))
    for c in range(CH):
        gaps[CORE + 2 * c].append(("U", c))
    for g in range(CORE, GAPS):
        for c in range(CH):
            for name, after in (("X2T", 6), ("OP", 4), ("OT", 3), ("T", 2)):
                if g == CORE + 2 * c + after:
                    gaps[g].append((name, c))
        for c in range(CH):
            if g - CORE - 2 * c in (0, 1):
                half = g - CORE - 2 * c
                gaps[g].append(("CORE", 2 * c + half))
    gaps[GAPS - 2].append(("LG", 0))
    gaps[GAPS - 1].append(("LGT", 0))
    return gaps


GAP = gap_products()
ORDER = []
for _products in GAP:
    for _name, _k in _products:
        if _name == "CORE":
            ORDER += [("A", 2 * _k), ("A", 2 * _k + 1)]
        elif _name not in ("LG", "LGT"):
            ORDER.append((_name, _k))
INDEX = {product: n for n, product in enumerate(ORDER)}
PER_BANK = len(ORDER) // 2
assert len(ORDER) % 2 == 0

ATT_MATS = ("q", "k", "v", "o")
NUM_STAGE = 2
CB_PER_TILE = 1 + NE + 2
OB_PER_TILE = CH + 1
ROUTER_STEPS = 23


def build(nc, x, w_att, w_up, w_down, w_gate, b_qk, b_vo, b_up, b_down, ident_in, causal_in, select_in, rank_in, out):
    with ExitStack() as ctx:
        def sb(name, shape, dtype=F32):
            return ctx.enter_context(nc.sbuf_tensor(name, shape, dtype))

        def sem(name):
            return ctx.enter_context(nc.semaphore(name))

        att_hi = [sb(f"w{m}_hi", [P, KC, D], F32R) for m in ATT_MATS]
        att_lo = [sb(f"w{m}_lo", [P, KC, D], F32R) for m in ATT_MATS]
        up_hi = sb("up_hi", [P, NE + 1, KC, HID], F32R)
        up_lo = sb("up_lo", [P, NE + 1, KC, HID], F32R)
        down_hi = sb("down_hi", [P, NE + 1, KC, D], F32R)
        down_lo = sb("down_lo", [P, NE + 1, KC, D], F32R)
        gate_hi = sb("gate_hi", [P, KC, P], F32R)
        gate_lo = sb("gate_lo", [P, KC, P], F32R)
        bdown_hi = sb("bdown_hi", [P, D], F32R)
        bdown_lo = sb("bdown_lo", [P, D], F32R)
        select = sb("select_r", [P, NE], F32R)
        stage = [sb(f"stage{i}", [P, KC * D]) for i in range(NUM_STAGE)]
        ident = sb("ident_sb", [P, P])
        causal = sb("causal_sb", [P, P])
        rank = sb("rank_sb", [P, CH, NE])
        select_f = sb("select_f", [P, NE])
        bqk = sb("bqk", [P, 2 * KC])
        bqk_minus = sb("bqk_minus", [P, 2 * KC])
        bvo = sb("bvo", [P, 2, D])
        bup = sb("bup", [P, (NE + 1) * KC])
        minus_half = sb("minus_half", [P, CH])
        x_in = sb("x_in", [P, CH, D])
        x2 = sb("x2", [P, 2, CH, D])
        xn_q = sb("xn_q", [P, CH * D])
        xn = xn_q[:, :].rearrange("p (c d) -> p c d", c=CH)
        q_map = xn_q[:, :].rearrange("p (k n) -> p k n", k=KC)
        xT_hi = sb("xT_hi", [P, KC, TOK], F32R)
        xT_lo = sb("xT_lo", [P, KC, TOK], F32R)
        q_diag = sb("q_diag", [P, 2, H, P])
        k_map = sb("k_map", [P, KC, TOK])
        k_tok = sb("k_tok", [P, CH, D])
        v_slot = sb("v_slot", [P, CH, H, SLOT])
        work = sb("work", [P, 2, TOK])
        state = sb("state", [P, 2, KC, HH * SLOT])
        carry = sb("carry", [P, 2, H, VW])
        o_slot = sb("o_slot", [P, TOK])
        den = sb("den", [P, H])
        rden = sb("rden", [P, H])
        o_tok = sb("o_tok", [P, D])
        oT_hi = sb("oT_hi", [P, KC, P], F32R)
        oT_lo = sb("oT_lo", [P, KC, P], F32R)
        x2n = sb("x2n", [P, D])
        x2T_hi = sb("x2T_hi", [P, 2, KC, TOK], F32R)
        x2T_lo = sb("x2T_lo", [P, 2, KC, TOK], F32R)
        stats = sb("stats", [P, CH, 6])
        mv = sb("mv", [P, CH, 2])
        var = sb("var", [P, CH])
        rstd = sb("rstd", [P, CH])
        r_e = sb("r_e", [P, CH, NE])
        r_p = sb("r_p", [P, CH, NE])
        r_a = sb("r_a", [P, CH, NE])
        r_b = sb("r_b", [P, CH, NE])
        r_first = sb("r_first", [P, CH, NE])
        r_rest = sb("r_rest", [P, CH, NE])
        r_s = sb("r_s", [P, 8, CH])
        comb = sb("comb", [P, CH, SLOT])
        combT = sb("combT", [P, TOK], F32R)
        h = sb("h", [P, KC, TOK])
        h_hi = sb("h_hi", [P, KC, TOK], F32R)
        h_lo = sb("h_lo", [P, KC, TOK], F32R)

        ab = [ctx.enter_context(nc.psum_tensor(f"ab{i}", [P, TOK], F32)) for i in range(2)]
        ob = ctx.enter_context(nc.psum_tensor("ob", [P, TOK], F32))
        cb = ctx.enter_context(nc.psum_tensor("cb", [P, TOK], F32))
        zb = [ctx.enter_context(nc.psum_tensor(f"zb{i}", [P, TOK], F32)) for i in range(KC)]
        yb = [ctx.enter_context(nc.psum_tensor(f"yb{i}", [P, TOK], F32)) for i in range(KC)]

        const_loaded = sem("const_loaded")
        stage_loaded = [sem(f"stage_loaded{i}") for i in range(NUM_STAGE)]
        mat_hi = sem("mat_hi")
        mat_lo = sem("mat_lo")
        zeroed = sem("zeroed")
        slots_set = sem("slots_set")
        small_hi = sem("small_hi")
        small_lo = sem("small_lo")
        x_loaded = sem("x_loaded")
        ln1_stats, ln1_mean, ln1_var = sem("ln1_stats"), sem("ln1_mean"), sem("ln1_var")
        ln1_rstd, xn_ready, x_biased = sem("ln1_rstd"), sem("xn_ready"), sem("x_biased")
        ab_full = [sem(f"ab_full{i}") for i in range(2)]
        ab_free = [sem(f"ab_free{i}") for i in range(2)]
        ob_free = sem("ob_free")
        ob_logits, ob_logitsT = sem("ob_logits"), sem("ob_logitsT")
        xT_hi_ready, oT_hi_ready, x2T_hi_ready = sem("xT_hi_ready"), sem("oT_hi_ready"), sem("x2T_hi_ready")
        below_ready, exp_ready = sem("below_ready"), sem("exp_ready")
        mapped = sem("mapped")
        q_spread = [sem(f"q_spread{i}") for i in range(2)]
        state_ready = sem("state_ready")
        group_done = sem("group_done")
        den_ready, rden_ready = sem("den_ready"), sem("rden_ready")
        ln2_stats, ln2_mean, ln2_var = sem("ln2_stats"), sem("ln2_mean"), sem("ln2_var")
        ln2_rstd, x2n_ready = sem("ln2_rstd"), sem("x2n_ready")
        router = sem("router")
        router_exp = sem("router_exp")
        combT_ready = sem("combT_ready")
        z_full = sem("z_full")
        h_ready = sem("h_ready")
        cb_full = sem("cb_full")
        h_scaled, h_hi_ready, h_lo_ready = sem("h_scaled"), sem("h_hi_ready"), sem("h_lo_ready")
        down_done = sem("down_done")
        y_ready = sem("y_ready")
        out_ready = sem("out_ready")
        out_stored = sem("out_stored")

        def f32(ap):
            return ap.bitcast(F32)

        primed = {id(s): n for s, n in ((y_ready, 1), (out_ready, 1), (cb_full, 1), (down_done, 1), (out_stored, 16))}

        def wait(eng, s, value):
            if not (isinstance(value, int) and value <= 0):
                eng.wait_ge(s, value + primed.get(id(s), 0))

        def part_from_wait(eng):
            eng.nop(nofuse=True)

        def bank(product):
            return ab[INDEX[product] % 2]

        def bank_is_free(eng, product, t):
            n = INDEX[product]
            wait(eng, ab_free[n % 2], PER_BANK * t + n // 2)

        def bank_is_full(eng, product, t):
            n = INDEX[product]
            wait(eng, ab_full[n % 2], PER_BANK * t + n // 2 + 1)

        def consumed(eng, product, t):
            n = INDEX[product]
            wait(eng, ab_free[n % 2], PER_BANK * t + n // 2 + 1)

        def other_bank(product, earlier):
            return INDEX[product] % 2 != INDEX[earlier] % 2

        def full_sem(product):
            return ab_full[INDEX[product] % 2]

        def free_sem(product):
            return ab_free[INDEX[product] % 2]

        mats = [(att_hi[i][:, :, :], att_lo[i][:, :, :], w_att[i]) for i in range(3)]
        mats.append((gate_hi[:, :, :], gate_lo[:, :, :], w_gate))
        mats.append((att_hi[3][:, :, :], att_lo[3][:, :, :], w_att[3]))
        NUM_ATT = len(mats)
        for e in range(NE + 1):
            mats.append((up_hi[:, e], up_lo[:, e], w_up[e]))
            mats.append((down_hi[:, e], down_lo[:, e], w_down[e]))

        def staged(n):
            width = mats[n][2].shape[2]
            return stage[n % NUM_STAGE][:, 0:KC * width].rearrange("p (k n) -> p k n", k=KC)

        def mats_of_gap(g):
            per = (len(mats) - NUM_ATT + GAPS - 3) // (GAPS - 2)
            first = NUM_ATT + per * g
            return range(min(first, len(mats)), min(first + per, len(mats)))

        block = ctx.enter_context(nc.Block())

        @block.sync
        def _(sp):
            x_rows = x.rearrange("(t c p) d -> t p c d", c=CH, p=P)
            out_rows = out.rearrange("(t c p) d -> t p c d", c=CH, p=P)
            consts = [(bqk[:, :], b_qk), (bvo[:, :, :], b_vo), (ident[:, :], ident_in), (causal[:, :], causal_in),
                      (select_f[:, :], select_in), (rank[:, :, :], rank_in), (bup[:, :], b_up)]

            def load_mat(n):
                if n >= NUM_STAGE:
                    sp.wait_ge(mat_lo, n - NUM_STAGE + 1)
                    sp.wait_ge(mat_hi, n - NUM_STAGE + 1)
                sp.dma_start(staged(n), mats[n][2]).then_inc(stage_loaded[n % NUM_STAGE], 16)

            def load_x(t):
                sp.dma_start(x_in[:, :, :], x_rows[t]).then_inc(x_loaded, 16)

            def spread_q(t, c):
                if c == 0:
                    wait(sp, mapped, 2 * KC * t + KC)
                    wait(sp, zeroed, 1)
                wait(sp, group_done, NG * CH * t + NG * (c - 1))
                for head in range(H):
                    k, r = head // HH, DH * (head % HH)
                    sp.dma_start(q_diag[r:r + DH, c % 2, head, :],
                                 q_map[r:r + DH, k, P * c:P * (c + 1)]).then_inc(q_spread[c % 2], 16)

            def attention(t):
                for c in range(CH):
                    spread_q(t, c)

            sp.sem_inc(y_ready, 1)
            sp.sem_inc(out_ready, 1)
            sp.sem_inc(cb_full, 1)
            sp.sem_inc(down_done, 1)
            sp.sem_inc(out_stored, 16)
            load_x(0)
            for n in range(2):
                load_mat(n)
            for dst, src in consts:
                sp.dma_start(dst, src).then_inc(const_loaded, 16)
            sp.wait_ge(zeroed, 1)
            sp.dma_start(h[:, 0, 0:D], b_down).then_inc(const_loaded, 16)
            for n in range(2, NUM_ATT):
                load_mat(n)
            for g in range(GAPS):
                for n in mats_of_gap(g):
                    load_mat(n)
                if g == 1:
                    spread_q(0, 0)
                    spread_q(0, 1)
                if g == CORE + 1:
                    spread_q(0, 2)
                if g == CORE + 3:
                    spread_q(0, 3)

            def store(t):
                wait(sp, out_ready, 2 * (t + 1))
                sp.dma_start(out_rows[t], x2[:, t % 2, :, :]).then_inc(out_stored, 16)

            def next_x(t):
                consumed(sp, ("OP", CH - 1), t - 1)
                load_x(t)

            next_x(1)
            with sp.Fori(1, NT - 1) as t:
                attention(t)
                next_x(t + 1)
                store(t - 1)
            attention(NT - 1)
            store(NT - 2)
            store(NT - 1)
            wait(sp, out_stored, 16 * NT)

        @block.gpsimd
        def _(pool):
            pool.memset(q_diag[:, :, :, :], 0.0)
            pool.memset(minus_half[:, :], -0.5)
            pool.memset(carry[:, :, :, :], 0.0)
            pool.memset(comb[:, :, :], 0.0)
            pool.memset(v_slot[:, :, :, :], 0.0)
            pool.memset(state[:, :, :, :], 0.0)
            pool.memset(f32(combT[:, :]), 0.0).then_inc(zeroed, 1)
            pool.wait_ge(zeroed, 1)

            def split_lo(n):
                pool.wait_ge(mat_hi, n + 1)
                pool.tensor_tensor(mats[n][1], staged(n), f32(mats[n][0]), ALU.subtract).then_inc(mat_lo, 1)

            def attention_gap(g, t):
                if g == 0:
                    wait(pool, ln1_var, t + 1)
                    pool.tensor_tensor(rstd[:, :], var[:, :], minus_half[:, :], ALU.pow).then_inc(ln1_rstd, 1)
                    wait(pool, xn_ready, t + 1)
                    pool.tensor_tensor(x_in[:, :, :], x_in[:, :, :],
                                       bvo[:, 1:2, :].to_broadcast([P, CH, D]), ALU.add).then_inc(x_biased, 1)
                for name, c in GAP[g]:
                    if name == "OP":
                        wait(pool, ln2_var, CH * t + c + 1)
                        pool.tensor_tensor(rstd[:, c:c + 1], var[:, c:c + 1], minus_half[:, c:c + 1],
                                           ALU.pow).then_inc(ln2_rstd, 1)

            for n in range(NUM_ATT):
                split_lo(n)
                if n == 0:
                    pool.wait_ge(const_loaded, 16 * 8)
            for g in range(GAPS):
                attention_gap(g, 0)
                for n in mats_of_gap(g):
                    split_lo(n)
            with pool.Fori(1, NT) as t:
                for g in range(GAPS):
                    attention_gap(g, t)

        @block.tensor
        def _(pe):
            def split_product(dst, w_hi, w_lo, x_hi, x_lo, first, last):
                pe.matmul(dst, w_hi, x_hi, start=first, stop=False)
                pe.matmul(dst, w_hi, x_lo, start=False, stop=False)
                return pe.matmul(dst, w_lo, x_hi, start=False, stop=last)

            def project(name, k, t):
                m = ATT_MATS.index(name.lower())
                bank_is_free(pe, (name, k), t)
                for kc in range(KC):
                    last = split_product(bank((name, k))[:, :], att_hi[m][:, kc, P * k:P * (k + 1)],
                                         att_lo[m][:, kc, P * k:P * (k + 1)], xT_hi[:, kc, :], xT_lo[:, kc, :],
                                         kc == 0, kc == KC - 1)
                last.then_inc(full_sem((name, k)), 1)

            def core(c, half, t):
                groups = (2 * half, 2 * half + 1)
                if half == 0:
                    if c % 2 == 0:
                        wait(pe, q_spread[0], 16 * H * (2 * t + c // 2 + 1))
                    else:
                        wait(pe, q_spread[1], 16 * H * (2 * t + c // 2 + 1))
                    wait(pe, mapped, 2 * KC * (t + 1))
                for g in groups:
                    k = g * HG // HH
                    bank_is_free(pe, ("A", NG * c + g), t)
                    pe.matmul(bank(("A", NG * c + g))[:, :], k_map[:, k, P * c:P * (c + 1)],
                              q_diag[:, c % 2, HG * g:HG * (g + 1), :], start=True, stop=True)\
                        .then_inc(full_sem(("A", NG * c + g)), 1)
                if half == 0:
                    wait(pe, ob_free, OB_PER_TILE * t + c)
                    if c == 0:
                        wait(pe, router, ROUTER_STEPS * t)
                        wait(pe, state_ready, t + 1)
                    elif other_bank(("A", NG * c), ("U", c - 1)):
                        consumed(pe, ("U", c - 1), t)
                for g in groups:
                    k = g * HG // HH
                    consumed(pe, ("A", NG * c + g), t)
                    for i in range(HG):
                        head = HG * g + i
                        dst = ob[SLOT * i:SLOT * (i + 1), P * g:P * (g + 1)]
                        at = SLOT * (head % HH)
                        pe.matmul(dst, state[:, c % 2, k, at:at + SLOT], q_diag[:, c % 2, head, :],
                                  start=True, stop=False)
                        last = pe.matmul(dst, v_slot[:, c, head, :], work[:, g % 2, P * i:P * (i + 1)],
                                         start=False, stop=True)
                    last.then_inc(group_done, 1)

            def attention_product(name, c, t):
                if name == "CORE":
                    core(c // 2, c % 2, t)
                    return
                if name in ("Q", "K"):
                    if (name, c) == ("Q", 0):
                        if isinstance(t, int) and t == 0:
                            pe.wait_ge(mat_lo, 2)
                        consumed(pe, ("LN1", 1), t)
                        consumed(pe, ("LN1", 0), t)
                    project(name, c, t)
                    return
                if name == "LG":
                    consumed(pe, ("X2T", CH - 1), t)
                    wait(pe, ob_free, OB_PER_TILE * t + CH)
                    for kc in range(KC):
                        last = split_product(ob[:, :], gate_hi[:, kc, :], gate_lo[:, kc, :],
                                             x2T_hi[:, t % 2, kc, :], x2T_lo[:, t % 2, kc, :],
                                             kc == 0, kc == KC - 1)
                    last.then_inc(ob_logits, 1)
                    return
                if name == "LGT":
                    wait(pe, ob_free, OB_PER_TILE * t + CH + 1)
                    part_from_wait(pe)
                    for j in range(CH):
                        last = pe.transpose(ob[:, NE * j:NE * (j + 1)], o_slot[0:NE, P * j:P * (j + 1)],
                                            ident[0:NE, 0:NE])
                    last.then_inc(ob_logitsT, 1)
                    return
                product = (name, c)
                dst = bank(product)
                if name == "LN1":
                    wait(pe, xn_ready, t + 1)
                    bank_is_free(pe, product, t)
                    for j in range(CH):
                        last = pe.transpose(dst[:, P * j:P * (j + 1)], xn[:, j, P * c:P * (c + 1)], ident[:, :])
                if name == "V":
                    bank_is_free(pe, product, t)
                    if isinstance(t, int) and t == 0:
                        pe.wait_ge(mat_lo, NUM_ATT)
                    for j in range(2):
                        at = P * (2 * c + j)
                        for kc in range(KC):
                            last = split_product(dst[:, D * j:D * (j + 1)], xT_hi[:, kc, at:at + P],
                                                 xT_lo[:, kc, at:at + P], att_hi[2][:, kc, :], att_lo[2][:, kc, :],
                                                 kc == 0, kc == KC - 1)
                if name == "KT":
                    wait(pe, mapped, 2 * KC * (t + 1))
                    bank_is_free(pe, product, t)
                    for j in range(2):
                        for k in range(KC):
                            at = P * (2 * c + j)
                            last = pe.transpose(dst[:, D * j + P * k:D * j + P * (k + 1)],
                                                k_map[:, k, at:at + P], ident[:, :])
                if name == "U":
                    for source in (("KT", c // 2),):
                        assert not other_bank(("KT", c // 2), ("V", c // 2))
                        if other_bank(product, source):
                            consumed(pe, source, t)
                    bank_is_free(pe, product, t)
                    for k in range(KC):
                        last = pe.matmul(dst[:, HH * VW * k:HH * VW * (k + 1)], k_tok[:, c, P * k:P * (k + 1)],
                                         v_slot[:, c, HH * k:HH * (k + 1), 0:VW], start=True, stop=True)
                if name == "T":
                    wait(pe, ob_free, OB_PER_TILE * t + c + 1)
                    bank_is_free(pe, product, t)
                    for g in range(NG):
                        last = pe.transpose(dst[:, P * g:P * (g + 1)], o_slot[:, P * g:P * (g + 1)], ident[:, :])
                if name == "OT":
                    if other_bank(product, ("T", c)):
                        consumed(pe, ("T", c), t)
                    bank_is_free(pe, product, t)
                    for k in range(KC):
                        last = pe.transpose(dst[:, P * k:P * (k + 1)], o_tok[:, P * k:P * (k + 1)], ident[:, :])
                if name == "OP":
                    if other_bank(product, ("OT", c)):
                        consumed(pe, ("OT", c), t)
                    bank_is_free(pe, product, t)
                    for kc in range(KC):
                        last = split_product(dst[:, 0:D], oT_hi[:, kc, :], oT_lo[:, kc, :],
                                             att_hi[3][:, kc, :], att_lo[3][:, kc, :], kc == 0, kc == KC - 1)
                if name == "X2T":
                    wait(pe, x2n_ready, CH * t + c + 1)
                    bank_is_free(pe, product, t)
                    for k in range(KC):
                        last = pe.transpose(dst[:, P * k:P * (k + 1)], x2n[:, P * k:P * (k + 1)], ident[:, :])
                last.then_inc(full_sem(product), 1)

            def attention_gap(g, t):
                for name, c in GAP[g]:
                    attention_product(name, c, t)

            def up(e, t):
                for m in range(KC):
                    if e == 0:
                        wait(pe, y_ready, KC * t)
                    else:
                        wait(pe, h_ready, KC * ((NE + 1) * t + e - 1) + m + 1)
                    for kc in range(KC):
                        last = split_product(zb[m][:, :], up_hi[:, e, kc, P * m:P * (m + 1)],
                                             up_lo[:, e, kc, P * m:P * (m + 1)], x2T_hi[:, t % 2, kc, :],
                                             x2T_lo[:, t % 2, kc, :], kc == 0, kc == KC - 1)
                    last.then_inc(z_full, 1)

            def share_transpose(t):
                wait(pe, router, ROUTER_STEPS * (t + 1))
                wait(pe, out_ready, 2 * t)
                for j in range(CH):
                    last = pe.transpose(cb[0:SLOT, P * j:P * (j + 1)], comb[:, j, :], ident[:, :])
                last.then_inc(cb_full, 1)

            def share_broadcast(e, t):
                if e > 0:
                    wait(pe, h_scaled, KC * (NE * t + e))
                pe.matmul(cb[:, :], select[:, e:e + 1].to_broadcast([P, P]), combT[:, :],
                          start=True, stop=True).then_inc(cb_full, 1)

            def down_bias(t):
                wait(pe, y_ready, KC * t)
                for m in range(KC):
                    pe.matmul(yb[m][:, :], bdown_hi[:, P * m:P * (m + 1)], combT[:, :], start=True, stop=False)
                    pe.matmul(yb[m][:, :], bdown_lo[:, P * m:P * (m + 1)], combT[:, :], start=False, stop=False)

            def down(e, t):
                for k in range(KC):
                    wait(pe, h_lo_ready, KC * (NE + 1) * t + KC * e + k + 1)
                    for m in range(KC):
                        last = split_product(yb[m][:, :], down_hi[:, e, k, P * m:P * (m + 1)],
                                             down_lo[:, e, k, P * m:P * (m + 1)], h_hi[:, k, :], h_lo[:, k, :],
                                             False, e == NE and k == KC - 1)
                last.then_inc(down_done, 1)

            def out_transpose(t):
                for j in range(2):
                    wait(pe, y_ready, KC * (t + 1))
                    if j == 0:
                        wait(pe, h_scaled, KC * NE * (t + 1))
                    else:
                        wait(pe, out_ready, 2 * t + 1)
                    for i in range(2):
                        for k in range(KC):
                            at = P * (2 * j + i)
                            last = pe.transpose(cb[:, D * i + P * k:D * i + P * (k + 1)], h[:, k, at:at + P],
                                                ident[:, :])
                    last.then_inc(cb_full, 1)

            def step(t_att, t_exp):
                for g in range(GAPS):
                    if t_att is not None:
                        attention_gap(g, t_att)
                    if t_exp is None:
                        continue
                    e = g // 2
                    if e <= NE and g % 2 == 0:
                        up(e, t_exp)
                        if e == 0:
                            share_transpose(t_exp)
                    if e <= NE and g % 2 == 1:
                        if e == 0:
                            wait(pe, combT_ready, t_exp + 1)
                        if e < NE:
                            share_broadcast(e, t_exp)
                        if e == 0:
                            down_bias(t_exp)
                        if e > 0:
                            down(e - 1, t_exp)
                    if g == GAPS - 2:
                        down(NE, t_exp)
                if t_exp is not None:
                    out_transpose(t_exp)

            pe.wait_ge(const_loaded, 16 * 8)
            pe.wait_ge(slots_set, 1)
            step(0, None)
            pe.wait_ge(mat_lo, len(mats))
            pe.wait_ge(small_lo, 1)
            pe.wait_ge(small_hi, 2)
            with pe.Fori(1, NT) as t:
                step(t, t - 1)
            step(None, NT - 1)

        @block.scalar
        def _(act):
            def split_hi(n):
                act.wait_ge(stage_loaded[n % NUM_STAGE], 16 * (n // NUM_STAGE + 1))
                act.activation(mats[n][0], staged(n), ACT.Copy).then_inc(mat_hi, 1)

            def attention_product(name, c, t):
                product = (name, c)
                if name == "LN1":
                    bank_is_full(act, product, t)
                    act.activation(xT_hi[:, c, :], bank(product)[:, :], ACT.Copy).then_inc(xT_hi_ready, 1)
                if name in ("Q", "K"):
                    n = KC * (name == "K") + c
                    bank_is_full(act, product, t)
                    wait(act, mapped, 2 * KC * t + n)
                    if n == 0:
                        wait(act, group_done, NG * CH * t)
                    act.activation(work[:, 0, :], bank(product)[:, :], ACT.Relu, scale=-1.0,
                                   bias=bqk_minus[:, n:n + 1]).then_inc(below_ready, 1)
                    act.activation(work[:, 1, :], bank(product)[:, :], ACT.Relu,
                                   bias=bqk[:, n:n + 1]).then_inc(free_sem(product), 1)
                    wait(act, below_ready, 2 * KC * t + n + 1)
                    act.activation(work[:, 0, :], work[:, 0, :], ACT.Exp, scale=-1.0).then_inc(exp_ready, 1)
                if name == "KT":
                    bank_is_full(act, product, t)
                    if c == 0:
                        if other_bank(product, ("U", CH - 1)):
                            bank_is_full(act, ("U", CH - 1), t - 1)
                    act.activation(k_tok[:, 2 * c:2 * c + 2, :], bank(product)[:, :].rearrange(
                        "p (j d) -> p j d", j=2), ACT.Copy).then_inc(free_sem(product), 1)
                if name == "CORE" and c % 2 == 1:
                    wait(act, group_done, NG * (CH * t + c // 2 + 1))
                    if c // 2 > 0:
                        bank_is_full(act, ("T", c // 2 - 1), t)
                    else:
                        wait(act, ob_logitsT, t)
                    act.activation(o_slot[:, :], ob[:, :], ACT.Copy).then_inc(ob_free, 1)
                if name == "OT":
                    bank_is_full(act, product, t)
                    if c > 0 and other_bank(product, ("OP", c - 1)):
                        bank_is_full(act, ("OP", c - 1), t)
                    act.activation(oT_hi[:, :, :], bank(product)[:, 0:D].rearrange("p (k n) -> p k n", k=KC),
                                   ACT.Copy).then_inc(oT_hi_ready, 1)
                if name == "X2T":
                    bank_is_full(act, product, t)
                    act.activation(x2T_hi[:, t % 2, :, P * c:P * (c + 1)],
                                   bank(product)[:, 0:D].rearrange("p (k n) -> p k n", k=KC),
                                   ACT.Copy).then_inc(x2T_hi_ready, 1)
                if name == "LG":
                    wait(act, ob_logits, t + 1)
                    bank_is_full(act, ("T", CH - 1), t)
                    act.activation(o_slot[0:NE, :], ob[0:NE, :], ACT.Copy).then_inc(ob_free, 1)
                if name == "LGT":
                    wait(act, router, ROUTER_STEPS * t + 2)
                    act.activation(r_e[:, :, :], r_a[:, :, :], ACT.Exp).then_inc(router_exp, 1)

            def attention_gap(g, t):
                for name, c in GAP[g]:
                    attention_product(name, c, t)

            def hidden(e, t):
                for m in range(KC):
                    wait(act, z_full, KC * ((NE + 1) * t + e) + m + 1)
                    if e > 0:
                        wait(act, h_lo_ready, KC * ((NE + 1) * t + e - 1) + m + 1)
                    else:
                        wait(act, cb_full, CB_PER_TILE * t)
                    act.activation(h[:, m, :], zb[m][:, :], ACT.Silu,
                                   bias=bup[:, KC * e + m:KC * e + m + 1]).then_inc(h_ready, 1)

            def hidden_hi(e, t):
                for m in range(KC):
                    if e < NE:
                        wait(act, h_scaled, KC * (NE * t + e) + m + 1)
                    else:
                        wait(act, h_ready, KC * ((NE + 1) * t + e) + m + 1)
                    wait(act, down_done, (NE + 1) * t + e)
                    act.activation(h_hi[:, m, :], h[:, m, :], ACT.Copy).then_inc(h_hi_ready, 1)

            def step(t_att, t_exp):
                for g in range(GAPS):
                    if t_att is not None:
                        attention_gap(g, t_att)
                    if t_exp is None:
                        for n in mats_of_gap(g):
                            split_hi(n)
                        continue
                    e = g // 2
                    if e <= NE and g % 2 == 0:
                        hidden(e, t_exp)
                        if e == 0:
                            wait(act, cb_full, CB_PER_TILE * t_exp + 1)
                            act.activation(combT[0:SLOT, :], cb[0:SLOT, :], ACT.Copy).then_inc(combT_ready, 1)
                    if e <= NE and g % 2 == 1:
                        hidden_hi(e, t_exp)
                if t_exp is not None:
                    wait(act, down_done, (NE + 1) * (t_exp + 1))
                    wait(act, h_lo_ready, KC * (NE + 1) * (t_exp + 1))
                    for m in range(KC):
                        act.activation(h[:, m, :], yb[m][:, :], ACT.Copy).then_inc(y_ready, 1)

            for n in range(NUM_ATT):
                split_hi(n)
                if n == 0:
                    act.wait_ge(const_loaded, 16 * 8)
                    act.activation(select[:, :], select_f[:, :], ACT.Copy).then_inc(small_hi, 1)
                    act.activation(bdown_hi[:, :], h[:, 0, 0:D], ACT.Copy).then_inc(small_hi, 1)
            act.wait_ge(slots_set, 2)
            step(0, None)
            act.wait_ge(small_lo, 1)
            act.wait_ge(zeroed, 1)
            with act.Fori(1, NT) as t:
                step(t, t - 1)
            step(None, NT - 1)

        @block.vector
        def _(dve):
            def per_token(ap, n):
                return ap.unsqueeze(2).to_broadcast([P, CH, n])

            def norm_input(t):
                wait(dve, x_loaded, 16 * (t + 1))
                wait(dve, ln1_rstd, t)
                for c in range(CH):
                    last = dve.bn_stats(stats[:, c, :], x_in[:, c, :])
                last.then_inc(ln1_stats, 1)
                wait(dve, ln1_stats, t + 1)
                part_from_wait(dve)
                for c in range(CH):
                    last = dve.bn_aggr(mv[:, c, :], stats[:, c, :])
                last.then_inc(ln1_mean, 1)
                wait(dve, ln1_mean, t + 1)
                wait(dve, ln2_rstd, CH * t)
                dve.tensor_scalar(var[:, :], mv[:, :, 1], EPS_LN, None, ALU.add).then_inc(ln1_var, 1)
                wait(dve, ln1_rstd, t + 1)
                wait(dve, q_spread[0], 32 * H * t)
                wait(dve, q_spread[1], 32 * H * t)
                for c in range(CH):
                    last = dve.tensor_scalar(xn[:, c, :], x_in[:, c, :], mv[:, c, 0:1], rstd[:, c:c + 1],
                                             ALU.subtract, ALU.mult)
                last.then_inc(xn_ready, 1)

            def attention_product(name, c, t):
                product = (name, c)
                if name == "LN1":
                    wait(dve, xT_hi_ready, KC * t + c + 1)
                    dve.tensor_tensor(xT_lo[:, c, :], bank(product)[:, :], f32(xT_hi[:, c, :]),
                                      ALU.subtract).then_inc(free_sem(product), 1)
                if name in ("Q", "K"):
                    wait(dve, exp_ready, 2 * KC * t + KC * (name == "K") + c + 1)
                    if (name, c) == ("Q", 0):
                        bank_is_full(dve, ("LN1", 1), t)
                    dst = q_map if name == "Q" else k_map
                    dve.tensor_tensor(dst[:, c, :], work[:, 0, :], work[:, 1, :], ALU.add).then_inc(mapped, 1)
                if name == "V":
                    bank_is_full(dve, product, t)
                    if c == 0:
                        wait(dve, group_done, NG * CH * t)
                    dve.tensor_tensor(v_slot[:, 2 * c:2 * c + 2, :, 0:DH],
                                      bank(product)[:, :].rearrange("p (j h d) -> p j h d", j=2, h=H),
                                      bvo[:, 0:1, :].rearrange("p j (h d) -> p j h d", h=H).to_broadcast(
                                          [P, 2, H, DH]), ALU.add).then_inc(free_sem(product), 1)
                if name == "U":
                    if c == 0:
                        consumed(dve, ("U", CH - 1), t - 1)
                        wait(dve, group_done, NG * CH * t)
                        dve.tensor_copy(slots(0), carry[:, (t % TPB + TPB - 1) // TPB, :, :])\
                            .then_inc(state_ready, 1)
                        wait(dve, state_ready, t + 1)
                    else:
                        consumed(dve, ("U", c - 1), t)
                        wait(dve, group_done, NG * (CH * t + c))
                    bank_is_full(dve, product, t)
                    dst = slots((c + 1) % 2) if c < CH - 1 else carry[:, 1, :, :]
                    dve.tensor_tensor(dst, bank(product)[:, 0:H * VW].rearrange("p (h w) -> p h w", h=H),
                                      slots(c % 2), ALU.add).then_inc(free_sem(product), 1)
                if name == "CORE":
                    for i in range(2):
                        g = 2 * (c % 2) + i
                        n = NG * (c // 2) + g
                        bank_is_full(dve, ("A", n), t)
                        wait(dve, group_done, NG * CH * t + n - 1)
                        dve.tensor_tensor(work[:, g % 2, :].rearrange("p (i n) -> p i n", i=HG),
                                          bank(("A", n))[:, :].rearrange("p (i n) -> p i n", i=HG),
                                          causal[:, :].unsqueeze(1).to_broadcast([P, HG, P]),
                                          ALU.mult).then_inc(free_sem(("A", n)), 1)
                if name == "T":
                    n = CH * t + c + 1
                    bank_is_full(dve, product, t)
                    by_head = bank(product)[:, :].rearrange("p (h s) -> p h s", h=H)
                    dve.tensor_scalar(den[:, :], by_head[:, :, DH], EPS_DEN, None, ALU.max).then_inc(den_ready, 1)
                    wait(dve, den_ready, n)
                    dve.reciprocal(rden[:, :], den[:, :]).then_inc(rden_ready, 1)
                    wait(dve, rden_ready, n)
                    dve.tensor_tensor(o_tok[:, :].rearrange("p (h d) -> p h d", h=H), by_head[:, :, 0:DH],
                                      rden[:, :].unsqueeze(2).to_broadcast([P, H, DH]),
                                      ALU.mult).then_inc(free_sem(product), 1)
                if name == "OT":
                    wait(dve, oT_hi_ready, CH * t + c + 1)
                    dve.tensor_tensor(oT_lo[:, :, :], bank(product)[:, 0:D].rearrange("p (k n) -> p k n", k=KC),
                                      f32(oT_hi[:, :, :]), ALU.subtract).then_inc(free_sem(product), 1)
                if name == "OP":
                    n = CH * t + c + 1
                    bank_is_full(dve, product, t)
                    if c == 0:
                        wait(dve, x_biased, t + 1)
                        wait(dve, out_stored, 16 * (t - 1))
                    dve.tensor_tensor(x2[:, t % 2, c, :], bank(product)[:, 0:D], x_in[:, c, :],
                                      ALU.add).then_inc(free_sem(product), 1)
                    consumed(dve, product, t)
                    part_from_wait(dve)
                    dve.bn_stats(stats[:, c, :], x2[:, t % 2, c, :]).then_inc(ln2_stats, 1)
                    wait(dve, ln2_stats, n)
                    part_from_wait(dve)
                    dve.bn_aggr(mv[:, c, :], stats[:, c, :]).then_inc(ln2_mean, 1)
                    wait(dve, ln2_mean, n)
                    dve.tensor_scalar(var[:, c:c + 1], mv[:, c, 1:2], EPS_LN, None, ALU.add).then_inc(ln2_var, 1)
                if name == "X2T":
                    wait(dve, x2T_hi_ready, CH * t + c + 1)
                    dve.tensor_tensor(x2T_lo[:, t % 2, :, P * c:P * (c + 1)],
                                      bank(product)[:, 0:D].rearrange("p (k n) -> p k n", k=KC),
                                      f32(x2T_hi[:, t % 2, :, P * c:P * (c + 1)]),
                                      ALU.subtract).then_inc(free_sem(product), 1)
                if name == "LGT":
                    route(t)

            def slots(i):
                return state[:, i, :, :].rearrange("p k (h s) -> p (k h) s", s=SLOT)[:, :, 0:VW]

            def norm_residual(c, t):
                n = CH * t + c + 1
                wait(dve, ln2_rstd, n)
                if c > 0:
                    bank_is_full(dve, ("X2T", c - 1), t)
                dve.tensor_scalar(x2n[:, :], x2[:, t % 2, c, :], mv[:, c, 0:1], rstd[:, c:c + 1],
                                  ALU.subtract, ALU.mult).then_inc(x2n_ready, 1)

            def route(t):
                done = [0]

                def then(ins):
                    done[0] += 1
                    ins.then_inc(router, 1)
                    wait(dve, router, ROUTER_STEPS * t + done[0])

                lgT = ob[:, 0:CH * NE].rearrange("p (c e) -> p c e", c=CH)
                m, s, rs, p1, at1, p2, at2, tot = (r_s[:, i, :] for i in range(8))
                wait(dve, ob_logitsT, t + 1)
                then(dve.tensor_reduce(m, lgT, AX_X, ALU.max))
                then(dve.tensor_tensor(r_a[:, :, :], lgT, per_token(m, NE), ALU.subtract))
                wait(dve, router_exp, t + 1)
                then(dve.tensor_reduce(s, r_e[:, :, :], AX_X, ALU.add))
                then(dve.reciprocal(rs, s))
                then(dve.tensor_tensor(r_p[:, :, :], r_e[:, :, :], per_token(rs, NE), ALU.mult))
                then(dve.tensor_reduce(p1, r_p[:, :, :], AX_X, ALU.max))
                then(dve.tensor_tensor(r_b[:, :, :], r_p[:, :, :], per_token(p1, NE), ALU.is_equal))
                then(dve.tensor_tensor(r_b[:, :, :], r_b[:, :, :], rank[:, :, :], ALU.mult))
                then(dve.tensor_reduce(at1, r_b[:, :, :], AX_X, ALU.max))
                then(dve.tensor_tensor(r_first[:, :, :], r_b[:, :, :], per_token(at1, NE), ALU.is_equal))
                then(dve.scalar_tensor_tensor(out=r_rest[:, :, :], in0=r_first[:, :, :], scalar=-2.0,
                                              in1=r_p[:, :, :], op0=ALU.mult, op1=ALU.add))
                then(dve.tensor_reduce(p2, r_rest[:, :, :], AX_X, ALU.max))
                then(dve.tensor_tensor(r_b[:, :, :], r_rest[:, :, :], per_token(p2, NE), ALU.is_equal))
                then(dve.tensor_tensor(r_b[:, :, :], r_b[:, :, :], rank[:, :, :], ALU.mult))
                then(dve.tensor_reduce(at2, r_b[:, :, :], AX_X, ALU.max))
                then(dve.tensor_tensor(r_b[:, :, :], r_b[:, :, :], per_token(at2, NE), ALU.is_equal))
                then(dve.tensor_tensor(r_b[:, :, :], r_b[:, :, :], r_first[:, :, :], ALU.add))
                then(dve.tensor_tensor(r_b[:, :, :], r_b[:, :, :], r_p[:, :, :], ALU.mult))
                then(dve.scalar_tensor_tensor(out=tot, in0=p1, scalar=1e-20, in1=p2, op0=ALU.add, op1=ALU.add))
                then(dve.reciprocal(rs, tot))
                then(dve.tensor_tensor(r_b[:, :, :], r_b[:, :, :], per_token(rs, NE), ALU.mult))
                wait(dve, cb_full, CB_PER_TILE * (t - 1) + 1)
                then(dve.tensor_copy(comb[:, :, 0:NE].bitcast(F32R), r_b[:, :, :]))
                then(dve.tensor_tensor(comb[:, :, NE:2 * NE].bitcast(F32R), r_b[:, :, :], comb[:, :, 0:NE],
                                       ALU.subtract))
                assert done[0] == ROUTER_STEPS

            def attention_gap(g, t):
                if g == 0:
                    norm_input(t)
                for c in range(CH):
                    if g == CORE + 2 * c + 5:
                        norm_residual(c, t)
                for name, c in GAP[g]:
                    attention_product(name, c, t)

            def scale_and_lo(e, t):
                for m in range(KC):
                    if e < NE:
                        n = KC * ((NE + 1) * t + e) + m
                        wait(dve, h_ready, n + 1)
                        if m == 0:
                            wait(dve, cb_full, CB_PER_TILE * t + 2 + e)
                        ins = dve.tensor_tensor(h[:, m, :], cb[:, :], h[:, m, :], ALU.mult)
                        ins.then_inc(h_scaled, 1)
                for m in range(KC):
                    n = KC * ((NE + 1) * t + e) + m
                    wait(dve, h_hi_ready, n + 1)
                    wait(dve, down_done, (NE + 1) * t + e)
                    dve.tensor_tensor(h_lo[:, m, :], h[:, m, :], f32(h_hi[:, m, :]),
                                      ALU.subtract).then_inc(h_lo_ready, 1)

            def add_residual(t):
                for j in range(2):
                    wait(dve, cb_full, CB_PER_TILE * t + 2 + NE + j)
                    at = x2[:, t % 2, 2 * j:2 * j + 2, :]
                    dve.tensor_tensor(at, cb[:, :].rearrange("p (j d) -> p j d", j=2), at,
                                      ALU.add).then_inc(out_ready, 1)

            def step(t_att, t_exp):
                for g in range(GAPS):
                    if t_att is not None:
                        attention_gap(g, t_att)
                    if t_exp is not None and g // 2 <= NE and g % 2 == 1:
                        scale_and_lo(g // 2, t_exp)
                if t_exp is not None:
                    add_residual(t_exp)

            dve.wait_ge(zeroed, 1)
            dve.memset(v_slot[:, :, :, DH:VW], 1.0)
            dve.memset(comb[:, :, 2 * NE:2 * NE + 1], 1.0).then_inc(slots_set, 1)
            dve.wait_ge(const_loaded, 16 * 8)
            dve.tensor_scalar(bqk_minus[:, :], bqk[:, :], -1.0, None, ALU.mult).then_inc(slots_set, 1)
            dve.wait_ge(small_hi, 2)
            dve.tensor_tensor(bdown_lo[:, :], h[:, 0, 0:D], f32(bdown_hi[:, :]), ALU.subtract).then_inc(small_lo, 1)
            step(0, None)
            with dve.Fori(1, NT) as t:
                step(t, t - 1)
            step(None, NT - 1)


def kernel(**inputs):
    import numpy as np
    import concourse.bacc as bacc
    from concourse.bass_utils import run_bass_kernel_spmd as run

    a = {k: np.ascontiguousarray(v) for k, v in inputs.items()}

    def by_rows(w):
        w = w.reshape(w.shape[:-2] + (KC, P, w.shape[-1]))
        return np.ascontiguousarray(np.swapaxes(w, -3, -2))

    gate = np.zeros((D, P), np.float32)
    gate[:, :NE] = a["L0_ffn_gate_w"].T
    b_down = np.zeros((P, D), np.float32)
    b_down[0:NE] = a["L0_ffn_down_b"]
    b_down[NE:2 * NE] = a["L0_ffn_down_b"]
    b_down[2 * NE] = a["L0_ffn_sh_down_b"]
    select = np.zeros((P, NE), np.float32)
    for e in range(NE):
        select[[e, NE + e], e] = 1.0
    b_up = np.concatenate([a["L0_ffn_up_b"], a["L0_ffn_sh_up_b"][None]])
    arrays = {
        "in_x": a["L0_attn_x"].reshape(B * T, D),
        "in_w_att": by_rows(np.stack([a[f"L0_attn_W{m}"].T for m in ATT_MATS])),
        "in_w_up": by_rows(np.concatenate([a["L0_ffn_up_w"], a["L0_ffn_sh_up_w"][None]])),
        "in_w_down": by_rows(np.concatenate([a["L0_ffn_down_w"], a["L0_ffn_sh_down_w"][None]])),
        "in_w_gate": by_rows(gate),
        "in_b_qk": np.ascontiguousarray(np.concatenate([a["L0_attn_bq"].reshape(KC, P), a["L0_attn_bk"].reshape(KC, P)]).T),
        "in_b_vo": np.ascontiguousarray(np.broadcast_to(np.stack([a["L0_attn_bv"], a["L0_attn_bo"]]), (P, 2, D))),
        "in_b_up": np.ascontiguousarray(b_up.reshape((NE + 1) * KC, P).T),
        "in_b_down": b_down,
        "in_ident": np.eye(P, dtype=np.float32),
        "in_causal": np.triu(np.ones((P, P), np.float32)),
        "in_select": select,
        "in_rank": np.ascontiguousarray(np.broadcast_to(np.arange(NE, 0, -1, dtype=np.float32), (P, CH, NE))),
    }
    nc = bacc.Bacc("TRN2", target_bir_lowering=False, num_devices=1)
    args = [nc.dram_tensor(name, v.shape, mybir.dt.from_np(v.dtype), kind="ExternalInput").ap()
            for name, v in arrays.items()]
    out = nc.dram_tensor("out", (B * T, D), F32, kind="ExternalOutput").ap()
    build(nc, *args[:5], args[5], args[6], args[7], args[8], *args[9:], out)
    r = run(nc, [arrays], core_ids=[0])
    return r.results[0]["out"].reshape(B, T, D)
```

```python
from contextlib import ExitStack

import concourse.bass as bass
from concourse import mybir

P = 128
ALU = mybir.AluOpType
ACT = mybir.ActivationFunctionType
AX_X = mybir.AxisListType.X
F32 = mybir.dt.float32
F32R = mybir.dt.float32r

B, T, D = 2, 2048, 256
H, DH = 16, 16
NE = 8
HID = 256
TOK = 512
CH = TOK // P
NT = B * T // TOK
TPB = T // TOK
KC = D // P
HG = 4
NG = H // HG
HH = H // KC
SLOT = 32
VW = DH + 1
EPS_LN = 1e-5
EPS_DEN = 1e-6

GAP = [
    [("CORE", 0)],
    [("CORE", 1), ("U", 0)],
    [("CORE", 2), ("T", 0)],
    [("CORE", 3), ("U", 1), ("OT", 0)],
    [("CORE", 4), ("T", 1), ("OP", 0)],
    [("CORE", 5), ("U", 2), ("OT", 1)],
    [("CORE", 6), ("T", 2), ("OP", 1)],
    [("CORE", 7), ("U", 3), ("OT", 2), ("X2T", 0)],
    [("T", 3), ("OP", 2), ("X2T", 1)],
    [("OT", 3)],
    [("X2T", 2), ("OP", 3)],
    [("LN1", 0), ("LN1", 1)],
    [("X2T", 3), ("Q", 0)],
    [("LG", 0), ("Q", 1)],
    [("LGT", 0), ("K", 0)],
    [("K", 1), ("REXP", 0), ("EXP", 0)],
    [("MAP", 0), ("V", 0)],
    [("V", 1)],
    [("KT", 0)],
    [("KT", 1)],
]
GAPS = len(GAP)
FRONT = ("LN1", "Q", "K", "EXP", "MAP", "V", "KT")
FRONT_ORDER = [p for products in GAP for p in products if p[0] in FRONT]
NO_BANK = ("LG", "LGT", "EXP", "REXP", "MAP")
STATS_AT = 8
BEFORE_LN1 = 10
ROUTE_AT = 16


def assign_banks():
    bank_of, place, count, last = {}, {}, [0, 0], 1
    for products in GAP:
        for name, k in products:
            if name in NO_BANK:
                continue
            for product in ([("A", 2 * k), ("A", 2 * k + 1)] if name == "CORE" else [(name, k)]):
                last = k % 2 if product in FRONT_ORDER else 1 - last
                bank_of[product] = last
                place[product] = count[last]
                count[last] += 1
    return bank_of, place, count


BANK, PLACE, PER_STEP = assign_banks()
FRONT_BANKED = [p for p in FRONT_ORDER if p[0] not in NO_BANK]
FIRST = {p: [q for q in FRONT_BANKED if BANK[q] == BANK[p]].index(p) for p in FRONT_BANKED}
FIRST_COUNT = [len([q for q in FRONT_BANKED if BANK[q] == b]) for b in range(2)]

ATT_MATS = ("q", "k", "v", "o")
NUM_STAGE = 2
CB_PER_TILE = 1 + NE
OB_PER_TILE = CH + 1
ROUTER_STEPS = 23


def build(nc, x, w_att, w_up, w_down, w_gate, b_qk, b_vo, b_up, b_down, ident_in, causal_in, select_in, rank_in, out):
    with ExitStack() as ctx:
        def sb(name, shape, dtype=F32):
            return ctx.enter_context(nc.sbuf_tensor(name, shape, dtype))

        def sem(name):
            return ctx.enter_context(nc.semaphore(name))

        att_hi = [sb(f"w{m}_hi", [P, KC, D], F32R) for m in ATT_MATS]
        att_lo = [sb(f"w{m}_lo", [P, KC, D], F32R) for m in ATT_MATS]
        up_hi = sb("up_hi", [P, NE + 1, KC, HID], F32R)
        up_lo = sb("up_lo", [P, NE + 1, KC, HID], F32R)
        down_hi = sb("down_hi", [P, NE + 1, KC, D], F32R)
        down_lo = sb("down_lo", [P, NE + 1, KC, D], F32R)
        gate_hi = sb("gate_hi", [P, KC, P], F32R)
        gate_lo = sb("gate_lo", [P, KC, P], F32R)
        bdown_hi = sb("bdown_hi", [P, D], F32R)
        bdown_lo = sb("bdown_lo", [P, D], F32R)
        select = sb("select_r", [P, NE], F32R)
        stage = [sb(f"stage{i}", [P, KC * D]) for i in range(NUM_STAGE)]
        ident = sb("ident_sb", [P, P])
        causal = sb("causal_sb", [P, P])
        rank = sb("rank_sb", [P, CH, NE])
        select_f = sb("select_f", [P, NE])
        bqk = sb("bqk", [P, 2 * KC])
        bqk_minus = sb("bqk_minus", [P, 2 * KC])
        bvo = sb("bvo", [P, 2, D])
        bup = sb("bup", [P, (NE + 1) * KC])
        minus_half = sb("minus_half", [P, CH])
        x_in = sb("x_in", [P, 2, CH, D])
        x2 = sb("x2", [P, 2, CH, D])
        xn_q = sb("xn_q", [P, CH * D])
        xn = xn_q[:, :].rearrange("p (c d) -> p c d", c=CH)
        q_map = xn_q[:, :].rearrange("p (k n) -> p k n", k=KC)
        xT_hi = sb("xT_hi", [P, KC, TOK], F32R)
        xT_lo = sb("xT_lo", [P, KC, TOK], F32R)
        q_diag = sb("q_diag", [P, 2, H, P])
        k_map = sb("k_map", [P, KC, TOK])[:, :, :]
        k_tok = sb("k_tok", [P, CH, D])
        v_slot = sb("v_slot", [P, CH, H, SLOT])
        work = sb("work", [P, 2, TOK])
        above = {"Q": k_tok[:, :, :].rearrange("p (k j) d -> p k (j d)", k=KC), "K": work[:, :, :]}
        state = sb("state", [P, 2, KC, HH * SLOT])
        carry = sb("carry", [P, 2, H, VW])
        o_slot = sb("o_slot", [P, TOK])
        den = sb("den", [P, H])
        rden = sb("rden", [P, H])
        o_tok = sb("o_tok", [P, D])
        oT_hi = sb("oT_hi", [P, KC, P], F32R)
        oT_lo = sb("oT_lo", [P, KC, P], F32R)
        x2n = sb("x2n", [P, D])
        x2T_hi = sb("x2T_hi", [P, 2, KC, TOK], F32R)
        x2T_lo = sb("x2T_lo", [P, 2, KC, TOK], F32R)
        stats1, stats = sb("stats1", [P, CH, 6]), sb("stats", [P, CH, 6])
        mv1, mv = sb("mv1", [P, CH, 2]), sb("mv", [P, CH, 2])
        var1, var = sb("var1", [P, CH]), sb("var", [P, CH])
        rstd1, rstd = sb("rstd1", [P, CH]), sb("rstd", [P, CH])
        r_e = sb("r_e", [P, CH, NE])
        r_p = sb("r_p", [P, CH, NE])
        r_a = sb("r_a", [P, CH, NE])
        r_b = sb("r_b", [P, CH, NE])
        r_first = sb("r_first", [P, CH, NE])
        r_rest = sb("r_rest", [P, CH, NE])
        r_s = sb("r_s", [P, 8, CH])
        comb = sb("comb", [P, CH, SLOT])
        combT = sb("combT", [P, TOK], F32R)
        h = sb("h", [P, KC, TOK])
        h_hi = sb("h_hi", [P, KC, TOK], F32R)
        h_lo = sb("h_lo", [P, KC, TOK], F32R)

        ab = [ctx.enter_context(nc.psum_tensor(f"ab{i}", [P, TOK], F32)) for i in range(2)]
        ob = ctx.enter_context(nc.psum_tensor("ob", [P, TOK], F32))
        cb = ctx.enter_context(nc.psum_tensor("cb", [P, TOK], F32))
        zb = [ctx.enter_context(nc.psum_tensor(f"zb{i}", [P, TOK], F32)) for i in range(KC)]
        yb = [ctx.enter_context(nc.psum_tensor(f"yb{i}", [P, TOK], F32)) for i in range(KC)]

        const_loaded = sem("const_loaded")
        stage_loaded = [sem(f"stage_loaded{i}") for i in range(NUM_STAGE)]
        mat_hi = sem("mat_hi")
        mat_lo = sem("mat_lo")
        zeroed = sem("zeroed")
        slots_set = sem("slots_set")
        small_hi = sem("small_hi")
        small_lo = sem("small_lo")
        x_loaded = sem("x_loaded")
        ln1_stats, ln1_mean, ln1_var = sem("ln1_stats"), sem("ln1_mean"), sem("ln1_var")
        ln1_rstd, xn_ready, x_biased = sem("ln1_rstd"), sem("xn_ready"), sem("x_biased")
        ab_full = [sem(f"ab_full{i}") for i in range(2)]
        ab_free = [sem(f"ab_free{i}") for i in range(2)]
        ob_free = sem("ob_free")
        ob_logits, ob_logitsT = sem("ob_logits"), sem("ob_logitsT")
        xT_hi_ready, oT_hi_ready, x2T_hi_ready = sem("xT_hi_ready"), sem("oT_hi_ready"), sem("x2T_hi_ready")
        below_ready, exp_ready = sem("below_ready"), sem("exp_ready")
        mapped = sem("mapped")
        q_spread = [sem(f"q_spread{i}") for i in range(2)]
        state_ready = sem("state_ready")
        group_done = sem("group_done")
        den_ready, rden_ready = sem("den_ready"), sem("rden_ready")
        ln2_stats, ln2_mean, ln2_var = sem("ln2_stats"), sem("ln2_mean"), sem("ln2_var")
        ln2_rstd, x2n_ready = sem("ln2_rstd"), sem("x2n_ready")
        router = sem("router")
        router_exp = sem("router_exp")
        combT_ready = sem("combT_ready")
        z_full = sem("z_full")
        h_ready = sem("h_ready")
        cb_full = sem("cb_full")
        h_scaled, h_hi_ready, h_lo_ready = sem("h_scaled"), sem("h_hi_ready"), sem("h_lo_ready")
        down_done, y_summed = sem("down_done"), sem("y_summed")
        out_full = sem("out_full")
        y_ready = sem("y_ready")
        out_ready = sem("out_ready")
        out_stored = sem("out_stored")

        def f32(ap):
            return ap.bitcast(F32)

        primed = {id(s): n for s, n in ((y_ready, 1), (out_ready, 1), (out_full, 1), (down_done, 1), (y_summed, 1),
                                         (cb_full, 1), (out_stored, 16))}

        def after(s, signals):
            if isinstance(signals, int):
                signals = max(signals, 0)
            return signals + primed.get(id(s), 0)

        def part_from_wait(eng):
            eng.nop(nofuse=True)

        def bank(product):
            return ab[BANK[product]]

        def before(product, t):
            b = BANK[product]
            if product not in FRONT_ORDER:
                left_out = 0
                if isinstance(t, int) and t == NT - 1:
                    left_out = len([q for q in FRONT_BANKED if BANK[q] == b and PLACE[q] < PLACE[product]])
                return FIRST_COUNT[b] + PER_STEP[b] * t + PLACE[product] - left_out
            if isinstance(t, int) and t <= 0:
                return FIRST[product] if t == 0 else -1
            return FIRST_COUNT[b] + PER_STEP[b] * (t - 1) + PLACE[product]

        def at_free(product, t):
            n = before(product, t)
            return max(n, 0) if isinstance(n, int) else n

        def at_full(product, t):
            if isinstance(t, int) and t < 0:
                return 0
            return before(product, t) + 1

        def other_bank(product, earlier):
            return BANK[product] != BANK[earlier]

        def full_sem(product):
            return ab_full[BANK[product]]

        def free_sem(product):
            return ab_free[BANK[product]]

        mats = [(att_hi[i][:, :, :], att_lo[i][:, :, :], w_att[i]) for i in range(3)]
        mats.append((gate_hi[:, :, :], gate_lo[:, :, :], w_gate))
        mats.append((att_hi[3][:, :, :], att_lo[3][:, :, :], w_att[3]))
        NUM_ATT = len(mats)
        for e in range(NE + 1):
            mats.append((up_hi[:, e], up_lo[:, e], w_up[e]))
            mats.append((down_hi[:, e], down_lo[:, e], w_down[e]))

        def staged(n):
            width = mats[n][2].shape[2]
            return stage[n % NUM_STAGE][:, 0:KC * width].rearrange("p (k n) -> p k n", k=KC)

        def mats_of_gap(g):
            per = -(-(len(mats) - NUM_ATT) // (GAPS - 2))
            first = NUM_ATT + per * g
            return range(min(first, len(mats)), min(first + per, len(mats)))

        block = ctx.enter_context(nc.Block())

        @block.sync
        def _(sp):
            x_rows = x.rearrange("(t c p) d -> t p c d", c=CH, p=P)
            out_rows = out.rearrange("(t c p) d -> t p c d", c=CH, p=P)
            consts = [(bqk[:, :], b_qk), (bvo[:, :, :], b_vo), (ident[:, :], ident_in), (causal[:, :], causal_in),
                      (select_f[:, :], select_in), (rank[:, :, :], rank_in), (bup[:, :], b_up)]

            def load_mat(n):
                if n >= NUM_STAGE:
                    sp.wait_ge(mat_lo, n - NUM_STAGE + 1)
                    sp.wait_ge(mat_hi, n - NUM_STAGE + 1)
                sp.dma_start(staged(n), mats[n][2]).then_inc(stage_loaded[n % NUM_STAGE], 16)

            def load_x(t):
                sp.dma_start(x_in[:, t % 2, :, :], x_rows[t]).then_inc(x_loaded, 16)

            def spread_q(t, c):
                if c == 0:
                    sp.wait_ge(mapped, 2 * t + 1)
                    sp.wait_ge(zeroed, after(zeroed, 1))
                sp.wait_ge(group_done, after(group_done, NG * CH * t + NG * (c - 1)))
                for i in range(HH):
                    sp.dma_start(q_diag[DH * i:DH * (i + 1), c % 2, :, :].rearrange(
                        "p (k i) n -> p i k n", k=KC)[:, i, :, :],
                        q_map[DH * i:DH * (i + 1), :, P * c:P * (c + 1)]).then_inc(q_spread[c % 2], 16)

            def step(t_core, t_front, t_exp):
                spread_q(t_core, 2)
                spread_q(t_core, 3)
                if t_front is not None:
                    if not (isinstance(t_front, int) and t_front + 1 >= NT):
                        sp.wait_ge(free_sem(("OP", CH - 1)), at_full(("OP", CH - 1), t_core))
                        load_x(t_front + 1)
                    spread_q(t_front, 0)
                    spread_q(t_front, 1)
                if t_exp is not None:
                    store(t_exp)

            def store(t):
                sp.wait_ge(out_ready, after(out_ready, 2 * (t + 1)))
                sp.dma_start(out_rows[t], x2[:, t % 2, :, :]).then_inc(out_stored, 16)

            sp.sem_inc(y_ready, 1)
            sp.sem_inc(out_ready, 1)
            sp.sem_inc(cb_full, 1)
            sp.sem_inc(down_done, 1)
            sp.sem_inc(y_summed, 1)
            sp.sem_inc(out_full, 1)
            sp.sem_inc(out_stored, 16)
            load_x(0)
            for n in range(2):
                load_mat(n)
            for dst, src in consts:
                sp.dma_start(dst, src).then_inc(const_loaded, 16)
            sp.wait_ge(zeroed, 1)
            sp.dma_start(h[:, 0, 0:D], b_down).then_inc(const_loaded, 16)
            for n in range(2, NUM_ATT):
                load_mat(n)
            load_x(1)
            spread_q(0, 0)
            spread_q(0, 1)
            for g in range(GAPS):
                for n in mats_of_gap(g):
                    load_mat(n)
                if g == 2:
                    spread_q(0, 2)
                if g == 4:
                    spread_q(0, 3)
                if g == 11:
                    sp.wait_ge(free_sem(("OP", CH - 1)), at_full(("OP", CH - 1), 0))
                    load_x(2)
                if g == 17:
                    spread_q(1, 0)
                    spread_q(1, 1)
            with sp.Fori(1, NT - 2) as t:
                step(t, t + 1, t - 1)
            step(NT - 2, NT - 1, NT - 3)
            step(NT - 1, None, NT - 2)
            store(NT - 1)
            sp.wait_ge(out_stored, after(out_stored, 16 * NT))

        @block.gpsimd
        def _(pool):
            pool.memset(q_diag[:, :, :, :], 0.0)
            pool.memset(minus_half[:, :], -0.5)
            pool.memset(carry[:, :, :, :], 0.0)
            pool.memset(comb[:, :, :], 0.0)
            pool.memset(v_slot[:, :, :, :], 0.0)
            pool.memset(state[:, :, :, :], 0.0)
            pool.memset(f32(combT[:, :]), 0.0).then_inc(zeroed, 1)
            pool.wait_ge(zeroed, 1)

            def split_lo(n):
                pool.wait_ge(mat_hi, n + 1)
                pool.tensor_tensor(mats[n][1], staged(n), f32(mats[n][0]), ALU.subtract).then_inc(mat_lo, 1)

            def input_rstd(t):
                pool.wait_ge(ln1_var, t + 1)
                pool.tensor_tensor(rstd1[:, :], var1[:, :], minus_half[:, :], ALU.pow).then_inc(ln1_rstd, 1)

            def bias_input(t):
                pool.wait_ge(xn_ready, t + 1)
                pool.tensor_tensor(x_in[:, t % 2, :, :], x_in[:, t % 2, :, :],
                                   bvo[:, 1:2, :].to_broadcast([P, CH, D]), ALU.add).then_inc(x_biased, 1)

            def step(t_core, t_front, t_exp):
                for g in range(GAPS):
                    for name, c in GAP[g]:
                        if name == "OP" and t_core is not None:
                            pool.wait_ge(ln2_var, CH * t_core + c + 1)
                            pool.tensor_tensor(rstd[:, c:c + 1], var[:, c:c + 1], minus_half[:, c:c + 1],
                                               ALU.pow).then_inc(ln2_rstd, 1)
                    if g == STATS_AT and t_front is not None:
                        input_rstd(t_front)
                    if g == BEFORE_LN1 and t_front is not None:
                        bias_input(t_front)
                    if t_exp is None:
                        for n in mats_of_gap(g):
                            split_lo(n)

            for n in range(NUM_ATT):
                split_lo(n)
                if n == 0:
                    pool.wait_ge(const_loaded, 16 * 8)
                    input_rstd(0)
            bias_input(0)
            step(0, 1, None)
            with pool.Fori(1, NT - 1) as t:
                step(t, t + 1, t - 1)
            step(NT - 1, None, NT - 2)

        @block.tensor
        def _(pe):
            def split_product(dst, w_hi, w_lo, x_hi, x_lo, first, last):
                pe.matmul(dst, w_hi, x_hi, start=first, stop=False)
                pe.matmul(dst, w_hi, x_lo, start=False, stop=False)
                return pe.matmul(dst, w_lo, x_hi, start=False, stop=last)

            def project(name, k, t):
                m = ATT_MATS.index(name.lower())
                pe.wait_ge(free_sem((name, k)), at_free((name, k), t))
                for kc in range(KC):
                    last = split_product(bank((name, k))[:, :], att_hi[m][:, kc, P * k:P * (k + 1)],
                                         att_lo[m][:, kc, P * k:P * (k + 1)], xT_hi[:, kc, :], xT_lo[:, kc, :],
                                         kc == 0, kc == KC - 1)
                last.then_inc(full_sem((name, k)), 1)

            def core(c, half, t):
                groups = (2 * half, 2 * half + 1)
                if half == 0:
                    if c % 2 == 0:
                        pe.wait_ge(q_spread[0], 16 * HH * (2 * t + c // 2 + 1))
                    else:
                        pe.wait_ge(q_spread[1], 16 * HH * (2 * t + c // 2 + 1))
                    pe.wait_ge(mapped, 2 * (t + 1))
                for g in groups:
                    k = g * HG // HH
                    pe.wait_ge(free_sem(("A", NG * c + g)), at_free(("A", NG * c + g), t))
                    pe.matmul(bank(("A", NG * c + g))[:, :], k_map[:, k, P * c:P * (c + 1)],
                              q_diag[:, c % 2, HG * g:HG * (g + 1), :], start=True, stop=True)\
                        .then_inc(full_sem(("A", NG * c + g)), 1)
                if half == 0:
                    pe.wait_ge(ob_free, after(ob_free, OB_PER_TILE * t + c))
                    if c == 0:
                        pe.wait_ge(router, after(router, ROUTER_STEPS * t))
                        pe.wait_ge(state_ready, t + 1)
                    else:
                        pe.wait_ge(free_sem(("U", c - 1)), at_full(("U", c - 1), t))
                for g in groups:
                    k = g * HG // HH
                    for i in range(HG):
                        head = HG * g + i
                        at = SLOT * (head % HH)
                        pe.matmul(ob[SLOT * i:SLOT * (i + 1), P * g:P * (g + 1)], state[:, c % 2, k, at:at + SLOT],
                                  q_diag[:, c % 2, head, :], start=g == 0, stop=False, skip_group_check=True)
                for g in groups:
                    pe.wait_ge(free_sem(("A", NG * c + g)), at_full(("A", NG * c + g), t))
                    for i in range(HG):
                        last = pe.matmul(ob[SLOT * i:SLOT * (i + 1), P * g:P * (g + 1)],
                                         v_slot[:, c, HG * g + i, :], work[:, g % 2, P * i:P * (i + 1)],
                                         start=False, stop=True, skip_group_check=True)
                    last.then_inc(group_done, 1)

            def attention_product(name, c, t):
                if name in ("EXP", "REXP", "MAP"):
                    return
                if name == "CORE":
                    core(c // 2, c % 2, t)
                    return
                if name in ("Q", "K"):
                    if (name, c) == ("Q", 0):
                        if isinstance(t, int) and t == 0:
                            pe.wait_ge(mat_lo, 2)
                        pe.wait_ge(free_sem(("LN1", 1)), at_full(("LN1", 1), t))
                        pe.wait_ge(free_sem(("LN1", 0)), at_full(("LN1", 0), t))
                    project(name, c, t)
                    return
                if name == "LG":
                    pe.wait_ge(free_sem(("X2T", CH - 1)), at_full(("X2T", CH - 1), t))
                    pe.wait_ge(ob_free, OB_PER_TILE * t + CH)
                    for kc in range(KC):
                        last = split_product(ob[:, :], gate_hi[:, kc, :], gate_lo[:, kc, :],
                                             x2T_hi[:, t % 2, kc, :], x2T_lo[:, t % 2, kc, :],
                                             kc == 0, kc == KC - 1)
                    last.then_inc(ob_logits, 1)
                    return
                if name == "LGT":
                    pe.wait_ge(ob_free, OB_PER_TILE * t + CH + 1)
                    part_from_wait(pe)
                    for j in range(CH):
                        last = pe.transpose(ob[:, NE * j:NE * (j + 1)], o_slot[0:NE, P * j:P * (j + 1)],
                                            ident[0:NE, 0:NE])
                    last.then_inc(ob_logitsT, 1)
                    return
                product = (name, c)
                dst = bank(product)
                if name == "LN1":
                    pe.wait_ge(xn_ready, t + 1)
                    pe.wait_ge(free_sem(product), at_free(product, t))
                    for j in range(CH):
                        last = pe.transpose(dst[:, P * j:P * (j + 1)], xn[:, j, P * c:P * (c + 1)], ident[:, :])
                if name == "V":
                    pe.wait_ge(free_sem(product), at_free(product, t))
                    if isinstance(t, int) and t == 0:
                        pe.wait_ge(mat_lo, NUM_ATT)
                    for j in range(2):
                        at = P * (2 * c + j)
                        for kc in range(KC):
                            last = split_product(dst[:, D * j:D * (j + 1)], xT_hi[:, kc, at:at + P],
                                                 xT_lo[:, kc, at:at + P], att_hi[2][:, kc, :], att_lo[2][:, kc, :],
                                                 kc == 0, kc == KC - 1)
                if name == "KT":
                    pe.wait_ge(mapped, 2 * (t + 1))
                    pe.wait_ge(free_sem(product), at_free(product, t))
                    for j in range(2):
                        for k in range(KC):
                            at = P * (2 * c + j)
                            last = pe.transpose(dst[:, D * j + P * k:D * j + P * (k + 1)],
                                                k_map[:, k, at:at + P], ident[:, :])
                if name == "U":
                    for source in (("KT", c // 2),):
                        assert not other_bank(("KT", c // 2), ("V", c // 2))
                        if other_bank(product, source):
                            pe.wait_ge(free_sem(source), at_full(source, t))
                    pe.wait_ge(free_sem(product), at_free(product, t))
                    for k in range(KC):
                        last = pe.matmul(dst[:, HH * VW * k:HH * VW * (k + 1)], k_tok[:, c, P * k:P * (k + 1)],
                                         v_slot[:, c, HH * k:HH * (k + 1), 0:VW], start=True, stop=True)
                if name == "T":
                    pe.wait_ge(ob_free, OB_PER_TILE * t + c + 1)
                    pe.wait_ge(free_sem(product), at_free(product, t))
                    for g in range(NG):
                        last = pe.transpose(dst[:, P * g:P * (g + 1)], o_slot[:, P * g:P * (g + 1)], ident[:, :])
                if name == "OT":
                    if other_bank(product, ("T", c)):
                        pe.wait_ge(free_sem(("T", c)), at_full(("T", c), t))
                    pe.wait_ge(free_sem(product), at_free(product, t))
                    for k in range(KC):
                        last = pe.transpose(dst[:, P * k:P * (k + 1)], o_tok[:, P * k:P * (k + 1)], ident[:, :])
                if name == "OP":
                    if other_bank(product, ("OT", c)):
                        pe.wait_ge(free_sem(("OT", c)), at_full(("OT", c), t))
                    pe.wait_ge(free_sem(product), at_free(product, t))
                    for kc in range(KC):
                        last = split_product(dst[:, 0:D], oT_hi[:, kc, :], oT_lo[:, kc, :],
                                             att_hi[3][:, kc, :], att_lo[3][:, kc, :], kc == 0, kc == KC - 1)
                if name == "X2T":
                    pe.wait_ge(x2n_ready, CH * t + c + 1)
                    pe.wait_ge(free_sem(product), at_free(product, t))
                    for k in range(KC):
                        last = pe.transpose(dst[:, P * k:P * (k + 1)], x2n[:, P * k:P * (k + 1)], ident[:, :])
                last.then_inc(full_sem(product), 1)

            def attention_gap(g, t_core, t_front):
                for name, c in GAP[g]:
                    t = t_front if (name, c) in FRONT_ORDER else t_core
                    if t is not None:
                        attention_product(name, c, t)

            def up(e, t):
                for m in range(KC):
                    if e == 0:
                        pe.wait_ge(out_ready, after(out_ready, 2 * t))
                    else:
                        pe.wait_ge(h_ready, KC * ((NE + 1) * t + e - 1) + m + 1)
                    for kc in range(KC):
                        last = split_product(zb[m][:, :], up_hi[:, e, kc, P * m:P * (m + 1)],
                                             up_lo[:, e, kc, P * m:P * (m + 1)], x2T_hi[:, t % 2, kc, :],
                                             x2T_lo[:, t % 2, kc, :], kc == 0, kc == KC - 1)
                    last.then_inc(z_full, 1)

            def share_transpose(t):
                pe.wait_ge(router, ROUTER_STEPS * (t + 1))
                pe.wait_ge(down_done, after(down_done, NE * t))
                for j in range(CH):
                    last = pe.transpose(cb[0:SLOT, P * j:P * (j + 1)], comb[:, j, :], ident[:, :])
                last.then_inc(cb_full, 1)

            def share_broadcast(e, t):
                if e > 0:
                    pe.wait_ge(h_scaled, after(h_scaled, KC * (NE * t + e)))
                pe.matmul(cb[:, :], select[:, e:e + 1].to_broadcast([P, P]), combT[:, :],
                          start=True, stop=True).then_inc(cb_full, 1)

            def down_bias(t):
                pe.wait_ge(y_ready, after(y_ready, KC * t))
                for m in range(KC):
                    pe.matmul(yb[m][:, :], bdown_hi[:, P * m:P * (m + 1)], combT[:, :], start=True, stop=False)
                    pe.matmul(yb[m][:, :], bdown_lo[:, P * m:P * (m + 1)], combT[:, :], start=False, stop=False)

            def down(e, t):
                for k in range(KC):
                    pe.wait_ge(h_lo_ready, KC * (NE + 1) * t + KC * e + k + 1)
                    for m in range(KC):
                        last = split_product(yb[m][:, :], down_hi[:, e, k, P * m:P * (m + 1)],
                                             down_lo[:, e, k, P * m:P * (m + 1)], h_hi[:, k, :], h_lo[:, k, :],
                                             False, False)
                last.then_inc(down_done, 1)

            def down_last(t):
                pe.wait_ge(h_lo_ready, KC * (NE + 1) * (t + 1))
                for m in range(KC):
                    for k in range(KC):
                        last = split_product(yb[m][:, :], down_hi[:, NE, k, P * m:P * (m + 1)],
                                             down_lo[:, NE, k, P * m:P * (m + 1)], h_hi[:, k, :], h_lo[:, k, :],
                                             False, k == KC - 1)
                    last.then_inc(y_summed, 1)

            def out_transpose(t):
                for j in range(2):
                    if j == 0:
                        pe.wait_ge(h_ready, KC * (NE + 1) * (t + 1))
                    for i in range(2):
                        for k in range(KC):
                            pe.wait_ge(y_ready, after(y_ready, KC * t + k + 1))
                            at = P * (2 * j + i)
                            last = pe.transpose(zb[j][:, D * i + P * k:D * i + P * (k + 1)], h[:, k, at:at + P],
                                                ident[:, :])
                    last.then_inc(out_full, 1)

            def step(t_core, t_front, t_exp):
                for g in range(GAPS):
                    attention_gap(g, t_core, t_front)
                    if t_exp is None:
                        continue
                    e = g // 2
                    if e <= NE and g % 2 == 0:
                        up(e, t_exp)
                        if e == 0:
                            share_transpose(t_exp)
                    if e <= NE and g % 2 == 1:
                        if e == 0:
                            pe.wait_ge(combT_ready, t_exp + 1)
                        if e < NE:
                            share_broadcast(e, t_exp)
                        if e == 0:
                            down_bias(t_exp)
                        if e > 0:
                            down(e - 1, t_exp)
                    if g == GAPS - 1:
                        down_last(t_exp)
                        out_transpose(t_exp)

            pe.wait_ge(const_loaded, 16 * 8)
            pe.wait_ge(slots_set, 1)
            for name, c in FRONT_ORDER:
                attention_product(name, c, 0)
            step(0, 1, None)
            pe.wait_ge(mat_lo, len(mats))
            pe.wait_ge(small_lo, 1)
            pe.wait_ge(small_hi, 2)
            with pe.Fori(1, NT - 1) as t:
                step(t, t + 1, t - 1)
            step(NT - 1, None, NT - 2)
            step(None, None, NT - 1)

        @block.scalar
        def _(act):
            def split_hi(n):
                act.wait_ge(stage_loaded[n % NUM_STAGE], 16 * (n // NUM_STAGE + 1))
                act.activation(mats[n][0], staged(n), ACT.Copy).then_inc(mat_hi, 1)

            def attention_product(name, c, t):
                product = (name, c)
                if name == "LN1":
                    act.wait_ge(full_sem(product), at_full(product, t))
                    act.activation(xT_hi[:, c, :], bank(product)[:, :], ACT.Copy).then_inc(xT_hi_ready, 1)
                if name in ("Q", "K"):
                    n = KC * (name == "K") + c
                    act.wait_ge(full_sem(product), at_full(product, t))
                    below = (q_map if name == "Q" else k_map)[:, c, :]
                    act.activation(below, bank(product)[:, :], ACT.Relu, scale=-1.0,
                                   bias=bqk_minus[:, n:n + 1]).then_inc(below_ready, 1)
                    act.activation(above[name][:, c, :], bank(product)[:, :], ACT.Relu,
                                   bias=bqk[:, n:n + 1]).then_inc(free_sem(product), 1)
                if name == "EXP":
                    act.wait_ge(below_ready, 2 * KC * (t + 1))
                    for z in (q_map, k_map):
                        act.activation(z, z, ACT.Exp, scale=-1.0).then_inc(exp_ready, 1)
                if name == "KT":
                    act.wait_ge(full_sem(product), at_full(product, t))
                    if c == 0:
                        if other_bank(product, ("U", CH - 1)):
                            act.wait_ge(full_sem(("U", CH - 1)), at_full(("U", CH - 1), t - 1))
                    act.activation(k_tok[:, 2 * c:2 * c + 2, :], bank(product)[:, :].rearrange(
                        "p (j d) -> p j d", j=2), ACT.Copy).then_inc(free_sem(product), 1)
                if name == "CORE" and c % 2 == 1:
                    act.wait_ge(group_done, NG * (CH * t + c // 2 + 1))
                    if c // 2 > 0:
                        act.wait_ge(full_sem(("T", c // 2 - 1)), at_full(("T", c // 2 - 1), t))
                    else:
                        act.wait_ge(ob_logitsT, after(ob_logitsT, t))
                    act.activation(o_slot[:, :], ob[:, :], ACT.Copy).then_inc(ob_free, 1)
                if name == "OT":
                    act.wait_ge(full_sem(product), at_full(product, t))
                    if c > 0 and other_bank(product, ("OP", c - 1)):
                        act.wait_ge(full_sem(("OP", c - 1)), at_full(("OP", c - 1), t))
                    act.activation(oT_hi[:, :, :], bank(product)[:, 0:D].rearrange("p (k n) -> p k n", k=KC),
                                   ACT.Copy).then_inc(oT_hi_ready, 1)
                if name == "X2T":
                    act.wait_ge(full_sem(product), at_full(product, t))
                    act.activation(x2T_hi[:, t % 2, :, P * c:P * (c + 1)],
                                   bank(product)[:, 0:D].rearrange("p (k n) -> p k n", k=KC),
                                   ACT.Copy).then_inc(x2T_hi_ready, 1)
                if name == "LG":
                    act.wait_ge(ob_logits, t + 1)
                    act.wait_ge(full_sem(("T", CH - 1)), at_full(("T", CH - 1), t))
                    act.activation(o_slot[0:NE, :], ob[0:NE, :], ACT.Copy).then_inc(ob_free, 1)
                if name == "REXP":
                    act.wait_ge(router, after(router, ROUTER_STEPS * t + 2))
                    act.activation(r_e[:, :, :], r_a[:, :, :], ACT.Exp).then_inc(router_exp, 1)

            def attention_gap(g, t_core, t_front):
                for name, c in GAP[g]:
                    t = t_front if (name, c) in FRONT_ORDER else t_core
                    if t is not None:
                        attention_product(name, c, t)

            def hidden(e, t):
                for m in range(KC):
                    act.wait_ge(z_full, KC * ((NE + 1) * t + e) + m + 1)
                    if e > 0:
                        act.wait_ge(h_lo_ready, KC * ((NE + 1) * t + e - 1) + m + 1)
                    else:
                        act.wait_ge(out_full, after(out_full, 2 * t))
                    act.activation(h[:, m, :], zb[m][:, :], ACT.Silu,
                                   bias=bup[:, KC * e + m:KC * e + m + 1]).then_inc(h_ready, 1)

            def hidden_hi(e, t):
                for m in range(KC):
                    if e < NE:
                        act.wait_ge(h_scaled, KC * (NE * t + e) + m + 1)
                    else:
                        act.wait_ge(h_ready, KC * ((NE + 1) * t + e) + m + 1)
                    if e == 0:
                        act.wait_ge(y_summed, after(y_summed, KC * t))
                    else:
                        act.wait_ge(down_done, after(down_done, NE * t + e))
                    act.activation(h_hi[:, m, :], h[:, m, :], ACT.Copy).then_inc(h_hi_ready, 1)

            def step(t_core, t_front, t_exp):
                for g in range(GAPS):
                    attention_gap(g, t_core, t_front)
                    if t_exp is None:
                        for n in mats_of_gap(g):
                            split_hi(n)
                        continue
                    e = g // 2
                    if e > 0 and g % 2 == 0:
                        hidden_hi(e - 1, t_exp)
                    if e <= NE and g % 2 == 0:
                        hidden(e, t_exp)
                        if e == 0:
                            act.wait_ge(cb_full, after(cb_full, CB_PER_TILE * t_exp + 1))
                            act.activation(combT[0:SLOT, :], cb[0:SLOT, :], ACT.Copy).then_inc(combT_ready, 1)
                if t_exp is not None:
                    act.wait_ge(h_lo_ready, KC * (NE + 1) * (t_exp + 1))
                    for m in range(KC):
                        act.wait_ge(y_summed, after(y_summed, KC * t_exp + m + 1))
                        act.activation(h[:, m, :], yb[m][:, :], ACT.Copy).then_inc(y_ready, 1)

            for n in range(NUM_ATT):
                split_hi(n)
                if n == 0:
                    act.wait_ge(const_loaded, 16 * 8)
                    act.activation(select[:, :], select_f[:, :], ACT.Copy).then_inc(small_hi, 1)
                    act.activation(bdown_hi[:, :], h[:, 0, 0:D], ACT.Copy).then_inc(small_hi, 1)
            act.wait_ge(slots_set, 2)
            for name, c in FRONT_ORDER:
                attention_product(name, c, 0)
            step(0, 1, None)
            act.wait_ge(small_lo, 1)
            act.wait_ge(zeroed, 1)
            with act.Fori(1, NT - 1) as t:
                step(t, t + 1, t - 1)
            step(NT - 1, None, NT - 2)
            step(None, None, NT - 1)

        @block.vector
        def _(dve):
            def per_token(ap, n):
                return ap.unsqueeze(2).to_broadcast([P, CH, n])

            def input_stats(t):
                dve.wait_ge(x_loaded, 16 * (t + 1))
                dve.wait_ge(ln1_rstd, after(ln1_rstd, t))
                for c in range(CH):
                    last = dve.bn_stats(stats1[:, c, :], x_in[:, t % 2, c, :])
                last.then_inc(ln1_stats, 1)
                dve.wait_ge(ln1_stats, t + 1)
                part_from_wait(dve)
                for c in range(CH):
                    last = dve.bn_aggr(mv1[:, c, :], stats1[:, c, :])
                last.then_inc(ln1_mean, 1)
                dve.wait_ge(ln1_mean, t + 1)
                dve.tensor_scalar(var1[:, :], mv1[:, :, 1], EPS_LN, None, ALU.add).then_inc(ln1_var, 1)

            def norm_input(t):
                dve.wait_ge(ln1_rstd, t + 1)
                dve.wait_ge(q_spread[0], after(q_spread[0], 32 * HH * t))
                dve.wait_ge(q_spread[1], after(q_spread[1], 32 * HH * t))
                for c in range(CH):
                    last = dve.tensor_scalar(xn[:, c, :], x_in[:, t % 2, c, :], mv1[:, c, 0:1], rstd1[:, c:c + 1],
                                             ALU.subtract, ALU.mult)
                last.then_inc(xn_ready, 1)

            def attention_product(name, c, t):
                product = (name, c)
                if name == "LN1":
                    dve.wait_ge(xT_hi_ready, KC * t + c + 1)
                    dve.tensor_tensor(xT_lo[:, c, :], bank(product)[:, :], f32(xT_hi[:, c, :]),
                                      ALU.subtract).then_inc(free_sem(product), 1)
                if name == "MAP":
                    for i, (z, relu) in enumerate(((q_map, above["Q"]), (k_map, above["K"]))):
                        dve.wait_ge(exp_ready, 2 * t + i + 1)
                        dve.tensor_tensor(z, z, relu, ALU.add).then_inc(mapped, 1)
                if name == "V":
                    dve.wait_ge(full_sem(product), at_full(product, t))
                    if c == 0:
                        dve.wait_ge(group_done, after(group_done, NG * CH * t))
                    dve.tensor_tensor(v_slot[:, 2 * c:2 * c + 2, :, 0:DH],
                                      bank(product)[:, :].rearrange("p (j h d) -> p j h d", j=2, h=H),
                                      bvo[:, 0:1, :].rearrange("p j (h d) -> p j h d", h=H).to_broadcast(
                                          [P, 2, H, DH]), ALU.add).then_inc(free_sem(product), 1)
                if name == "U":
                    if c == 0:
                        dve.wait_ge(state_ready, t + 1)
                    else:
                        dve.wait_ge(free_sem(("U", c - 1)), at_full(("U", c - 1), t))
                        dve.wait_ge(group_done, after(group_done, NG * (CH * t + c)))
                    dve.wait_ge(full_sem(product), at_full(product, t))
                    dst = slots((c + 1) % 2) if c < CH - 1 else carry[:, 1, :, :]
                    dve.tensor_tensor(dst, bank(product)[:, 0:H * VW].rearrange("p (h w) -> p h w", h=H),
                                      slots(c % 2), ALU.add).then_inc(free_sem(product), 1)
                if name == "CORE":
                    for i in range(2):
                        g = 2 * (c % 2) + i
                        n = NG * (c // 2) + g
                        dve.wait_ge(full_sem(("A", n)), at_full(("A", n), t))
                        dve.wait_ge(group_done, after(group_done, NG * CH * t + n - 1))
                        dve.tensor_tensor(work[:, g % 2, :].rearrange("p (i n) -> p i n", i=HG),
                                          bank(("A", n))[:, :].rearrange("p (i n) -> p i n", i=HG),
                                          causal[:, :].unsqueeze(1).to_broadcast([P, HG, P]),
                                          ALU.mult).then_inc(free_sem(("A", n)), 1)
                if name == "T":
                    n = CH * t + c + 1
                    dve.wait_ge(full_sem(product), at_full(product, t))
                    by_head = bank(product)[:, :].rearrange("p (h s) -> p h s", h=H)
                    dve.tensor_scalar(den[:, :], by_head[:, :, DH], EPS_DEN, None, ALU.max).then_inc(den_ready, 1)
                    dve.wait_ge(den_ready, after(den_ready, n))
                    dve.reciprocal(rden[:, :], den[:, :]).then_inc(rden_ready, 1)
                    dve.wait_ge(rden_ready, after(rden_ready, n))
                    dve.tensor_tensor(o_tok[:, :].rearrange("p (h d) -> p h d", h=H), by_head[:, :, 0:DH],
                                      rden[:, :].unsqueeze(2).to_broadcast([P, H, DH]),
                                      ALU.mult).then_inc(free_sem(product), 1)
                if name == "OT":
                    dve.wait_ge(oT_hi_ready, CH * t + c + 1)
                    dve.tensor_tensor(oT_lo[:, :, :], bank(product)[:, 0:D].rearrange("p (k n) -> p k n", k=KC),
                                      f32(oT_hi[:, :, :]), ALU.subtract).then_inc(free_sem(product), 1)
                if name == "OP":
                    n = CH * t + c + 1
                    dve.wait_ge(full_sem(product), at_full(product, t))
                    if c == 0:
                        dve.wait_ge(x_biased, t + 1)
                        dve.wait_ge(out_stored, after(out_stored, 16 * (t - 1)))
                    dve.tensor_tensor(x2[:, t % 2, c, :], bank(product)[:, 0:D], x_in[:, t % 2, c, :],
                                      ALU.add).then_inc(free_sem(product), 1)
                    dve.wait_ge(free_sem(product), at_full(product, t))
                    part_from_wait(dve)
                    dve.bn_stats(stats[:, c, :], x2[:, t % 2, c, :]).then_inc(ln2_stats, 1)
                    dve.wait_ge(ln2_stats, after(ln2_stats, n))
                    part_from_wait(dve)
                    dve.bn_aggr(mv[:, c, :], stats[:, c, :]).then_inc(ln2_mean, 1)
                    dve.wait_ge(ln2_mean, after(ln2_mean, n))
                    dve.tensor_scalar(var[:, c:c + 1], mv[:, c, 1:2], EPS_LN, None, ALU.add).then_inc(ln2_var, 1)
                if name == "X2T":
                    dve.wait_ge(x2T_hi_ready, CH * t + c + 1)
                    dve.tensor_tensor(x2T_lo[:, t % 2, :, P * c:P * (c + 1)],
                                      bank(product)[:, 0:D].rearrange("p (k n) -> p k n", k=KC),
                                      f32(x2T_hi[:, t % 2, :, P * c:P * (c + 1)]),
                                      ALU.subtract).then_inc(free_sem(product), 1)
                if name == "LGT":
                    dve.wait_ge(ob_logitsT, t + 1)
                    route(0, t)

            def slots(i):
                return state[:, i, :, :].rearrange("p k (h s) -> p (k h) s", s=SLOT)[:, :, 0:VW]

            def take_state(t):
                dve.wait_ge(free_sem(("U", CH - 1)), at_full(("U", CH - 1), t - 1))
                dve.wait_ge(group_done, after(group_done, NG * CH * t))
                dve.tensor_copy(slots(0), carry[:, (t % TPB + TPB - 1) // TPB, :, :]).then_inc(state_ready, 1)

            def norm_residual(c, t):
                n = CH * t + c + 1
                dve.wait_ge(ln2_rstd, after(ln2_rstd, n))
                if c > 0:
                    dve.wait_ge(full_sem(("X2T", c - 1)), at_full(("X2T", c - 1), t))
                dve.tensor_scalar(x2n[:, :], x2[:, t % 2, c, :], mv[:, c, 0:1], rstd[:, c:c + 1],
                                  ALU.subtract, ALU.mult).then_inc(x2n_ready, 1)

            def route(part, t):
                done = [0, 2, 8, 16][part:part + 1]

                def then(ins):
                    done[0] += 1
                    ins.then_inc(router, 1)
                    dve.wait_ge(router, after(router, ROUTER_STEPS * t + done[0]))

                lgT = ob[:, 0:CH * NE].rearrange("p (c e) -> p c e", c=CH)
                m, s, rs, p1, at1, p2, at2, tot = (r_s[:, i, :] for i in range(8))
                if part == 0:
                    then(dve.tensor_reduce(m, lgT, AX_X, ALU.max))
                    then(dve.tensor_tensor(r_a[:, :, :], lgT, per_token(m, NE), ALU.subtract))
                if part == 1:
                    dve.wait_ge(router_exp, t + 1)
                    then(dve.tensor_reduce(s, r_e[:, :, :], AX_X, ALU.add))
                    then(dve.reciprocal(rs, s))
                    then(dve.tensor_tensor(r_p[:, :, :], r_e[:, :, :], per_token(rs, NE), ALU.mult))
                    then(dve.tensor_reduce(p1, r_p[:, :, :], AX_X, ALU.max))
                    then(dve.tensor_tensor(r_b[:, :, :], r_p[:, :, :], per_token(p1, NE), ALU.is_equal))
                    then(dve.tensor_tensor(r_b[:, :, :], r_b[:, :, :], rank[:, :, :], ALU.mult))
                if part == 2:
                    then(dve.tensor_reduce(at1, r_b[:, :, :], AX_X, ALU.max))
                    then(dve.tensor_tensor(r_first[:, :, :], r_b[:, :, :], per_token(at1, NE), ALU.is_equal))
                    then(dve.scalar_tensor_tensor(out=r_rest[:, :, :], in0=r_first[:, :, :], scalar=-2.0,
                                                  in1=r_p[:, :, :], op0=ALU.mult, op1=ALU.add))
                    then(dve.tensor_reduce(p2, r_rest[:, :, :], AX_X, ALU.max))
                    then(dve.tensor_tensor(r_b[:, :, :], r_rest[:, :, :], per_token(p2, NE), ALU.is_equal))
                    then(dve.tensor_tensor(r_b[:, :, :], r_b[:, :, :], rank[:, :, :], ALU.mult))
                    then(dve.tensor_reduce(at2, r_b[:, :, :], AX_X, ALU.max))
                    then(dve.tensor_tensor(r_b[:, :, :], r_b[:, :, :], per_token(at2, NE), ALU.is_equal))
                if part == 3:
                    then(dve.tensor_tensor(r_b[:, :, :], r_b[:, :, :], r_first[:, :, :], ALU.add))
                    then(dve.tensor_tensor(r_b[:, :, :], r_b[:, :, :], r_p[:, :, :], ALU.mult))
                    then(dve.scalar_tensor_tensor(out=tot, in0=p1, scalar=1e-20, in1=p2, op0=ALU.add, op1=ALU.add))
                    then(dve.reciprocal(rs, tot))
                    then(dve.tensor_tensor(r_b[:, :, :], r_b[:, :, :], per_token(rs, NE), ALU.mult))
                    dve.wait_ge(cb_full, after(cb_full, CB_PER_TILE * (t - 1) + 1))
                    then(dve.tensor_copy(comb[:, :, 0:NE].bitcast(F32R), r_b[:, :, :]))
                    then(dve.tensor_tensor(comb[:, :, NE:2 * NE].bitcast(F32R), r_b[:, :, :], comb[:, :, 0:NE],
                                           ALU.subtract))
                    assert done[0] == ROUTER_STEPS

            def attention_gap(g, t_core, t_front):
                if g == 0 and t_core is not None:
                    take_state(t_core)
                for name, c in GAP[g]:
                    t = t_front if (name, c) in FRONT_ORDER else t_core
                    if t is not None:
                        attention_product(name, c, t)
                if g + 1 < GAPS and t_core is not None:
                    for name, c in GAP[g + 1]:
                        if name == "X2T":
                            norm_residual(c, t_core)
                if g == STATS_AT and t_front is not None:
                    input_stats(t_front)
                if g == BEFORE_LN1 and t_front is not None:
                    norm_input(t_front)
                if ROUTE_AT <= g < ROUTE_AT + 3 and t_core is not None:
                    route(1 + g - ROUTE_AT, t_core)

            def scale(e, t):
                for m in range(KC):
                    n = KC * ((NE + 1) * t + e) + m
                    dve.wait_ge(h_ready, n + 1)
                    if m == 0:
                        dve.wait_ge(cb_full, after(cb_full, CB_PER_TILE * t + 2 + e))
                    dve.tensor_tensor(h[:, m, :], cb[:, :], h[:, m, :], ALU.mult).then_inc(h_scaled, 1)

            def hidden_lo(e, t):
                for m in range(KC):
                    n = KC * ((NE + 1) * t + e) + m
                    dve.wait_ge(h_hi_ready, n + 1)
                    if e == 0:
                        dve.wait_ge(y_summed, after(y_summed, KC * t))
                    else:
                        dve.wait_ge(down_done, after(down_done, NE * t + e))
                    dve.tensor_tensor(h_lo[:, m, :], h[:, m, :], f32(h_hi[:, m, :]),
                                      ALU.subtract).then_inc(h_lo_ready, 1)

            def add_residual(t):
                for j in range(2):
                    dve.wait_ge(out_full, after(out_full, 2 * t + j + 1))
                    at = x2[:, t % 2, 2 * j:2 * j + 2, :]
                    dve.tensor_tensor(at, zb[j][:, :].rearrange("p (j d) -> p j d", j=2), at,
                                      ALU.add).then_inc(out_ready, 1)

            def step(t_core, t_front, t_exp):
                for g in range(GAPS):
                    attention_gap(g, t_core, t_front)
                    if t_exp is None:
                        continue
                    if g > 0 and g % 2 == 0:
                        hidden_lo(g // 2 - 1, t_exp)
                    if g // 2 < NE and g % 2 == 1:
                        scale(g // 2, t_exp)
                if t_exp is not None:
                    add_residual(t_exp)

            dve.wait_ge(zeroed, 1)
            dve.memset(v_slot[:, :, :, DH:VW], 1.0)
            dve.memset(comb[:, :, 2 * NE:2 * NE + 1], 1.0).then_inc(slots_set, 1)
            dve.wait_ge(const_loaded, 16 * 8)
            dve.tensor_scalar(bqk_minus[:, :], bqk[:, :], -1.0, None, ALU.mult).then_inc(slots_set, 1)
            dve.wait_ge(small_hi, 2)
            dve.tensor_tensor(bdown_lo[:, :], h[:, 0, 0:D], f32(bdown_hi[:, :]), ALU.subtract).then_inc(small_lo, 1)
            input_stats(0)
            norm_input(0)
            for name, c in FRONT_ORDER:
                attention_product(name, c, 0)
            step(0, 1, None)
            with dve.Fori(1, NT - 1) as t:
                step(t, t + 1, t - 1)
            step(NT - 1, None, NT - 2)
            step(None, None, NT - 1)


def kernel(**inputs):
    import numpy as np
    import concourse.bacc as bacc
    from concourse.bass_utils import run_bass_kernel_spmd as run

    a = {k: np.ascontiguousarray(v) for k, v in inputs.items()}

    def by_rows(w):
        w = w.reshape(w.shape[:-2] + (KC, P, w.shape[-1]))
        return np.ascontiguousarray(np.swapaxes(w, -3, -2))

    gate = np.zeros((D, P), np.float32)
    gate[:, :NE] = a["L0_ffn_gate_w"].T
    b_down = np.zeros((P, D), np.float32)
    b_down[0:NE] = a["L0_ffn_down_b"]
    b_down[NE:2 * NE] = a["L0_ffn_down_b"]
    b_down[2 * NE] = a["L0_ffn_sh_down_b"]
    select = np.zeros((P, NE), np.float32)
    for e in range(NE):
        select[[e, NE + e], e] = 1.0
    b_up = np.concatenate([a["L0_ffn_up_b"], a["L0_ffn_sh_up_b"][None]])
    arrays = {
        "in_x": a["L0_attn_x"].reshape(B * T, D),
        "in_w_att": by_rows(np.stack([a[f"L0_attn_W{m}"].T for m in ATT_MATS])),
        "in_w_up": by_rows(np.concatenate([a["L0_ffn_up_w"], a["L0_ffn_sh_up_w"][None]])),
        "in_w_down": by_rows(np.concatenate([a["L0_ffn_down_w"], a["L0_ffn_sh_down_w"][None]])),
        "in_w_gate": by_rows(gate),
        "in_b_qk": np.ascontiguousarray(np.concatenate([a["L0_attn_bq"].reshape(KC, P), a["L0_attn_bk"].reshape(KC, P)]).T),
        "in_b_vo": np.ascontiguousarray(np.broadcast_to(np.stack([a["L0_attn_bv"], a["L0_attn_bo"]]), (P, 2, D))),
        "in_b_up": np.ascontiguousarray(b_up.reshape((NE + 1) * KC, P).T),
        "in_b_down": b_down,
        "in_ident": np.eye(P, dtype=np.float32),
        "in_causal": np.triu(np.ones((P, P), np.float32)),
        "in_select": select,
        "in_rank": np.ascontiguousarray(np.broadcast_to(np.arange(NE, 0, -1, dtype=np.float32), (P, CH, NE))),
    }
    nc = bacc.Bacc("TRN2", target_bir_lowering=False, num_devices=1)
    args = [nc.dram_tensor(name, v.shape, mybir.dt.from_np(v.dtype), kind="ExternalInput").ap()
            for name, v in arrays.items()]
    out = nc.dram_tensor("out", (B * T, D), F32, kind="ExternalOutput").ap()
    build(nc, *args[:5], args[5], args[6], args[7], args[8], *args[9:], out)
    r = run(nc, [arrays], core_ids=[0])
    return r.results[0]["out"].reshape(B, T, D)
```

```python
from contextlib import ExitStack

import concourse.bass as bass
from concourse import mybir

P = 128
ALU = mybir.AluOpType
ACT = mybir.ActivationFunctionType
AX_X = mybir.AxisListType.X
F32 = mybir.dt.float32
F32R = mybir.dt.float32r

B, T, D = 2, 2048, 256
H, DH = 16, 16
NE = 8
HID = 256
TOK = 512
CH = TOK // P
NT = B * T // TOK
TPB = T // TOK
KC = D // P
HG = 4
NG = H // HG
HH = H // KC
SLOT = 32
VW = DH + 1
EPS_LN = 1e-5
EPS_DEN = 1e-6

GAP = [
    [("CORE", 0), ("AV", 0)],
    [("CORE", 1), ("QS", 0), ("U", 0), ("AV", 1)],
    [("CORE", 2), ("T", 0), ("AV", 2)],
    [("CORE", 3), ("QS", 1), ("U", 1), ("OT", 0), ("AV", 3)],
    [("CORE", 4), ("OP", 0), ("T", 1), ("AV", 4)],
    [("CORE", 5), ("QS", 2), ("U", 2), ("OT", 1), ("AV", 5)],
    [("CORE", 6), ("OP", 1), ("T", 2), ("AV", 6)],
    [("CORE", 7), ("QS", 3), ("OT", 2), ("AV", 7), ("X2T", 0)],
    [("OP", 2), ("T", 3), ("U", 3)],
    [("X2T", 1), ("OT", 3)],
    [("OP", 3), ("LN1", 0), ("X2T", 2)],
    [("LN1", 1)],
    [("Q", 0), ("X2T", 3)],
    [("Q", 1), ("LG", 0)],
    [("LGT", 0), ("K", 0)],
    [("K", 1), ("REXP", 0), ("EXP", 0), ("EXP", 1)],
    [("MAP", 0), ("MAP", 1), ("V", 0)],
    [("V", 1)],
    [("KT", 0)],
    [("KT", 1)],
]
GAPS = len(GAP)
FRONT = ("LN1", "Q", "K", "EXP", "MAP", "V", "KT")
FRONT_ORDER = [p for products in GAP for p in products if p[0] in FRONT]
NO_BANK = ("QS", "AV", "LG", "LGT", "EXP", "REXP", "MAP")
STATS_AT = 5
BEFORE_LN1 = 9
SHARES_AT = 10
ROUTE_AT = (16, 18, 19)


def assign_banks():
    bank_of, place, count, last = {}, {}, [0, 0], 1
    for products in GAP:
        for name, k in products:
            if name in NO_BANK:
                continue
            for product in ([("A", 2 * k), ("A", 2 * k + 1)] if name == "CORE" else [(name, k)]):
                last = k % 2 if product in FRONT_ORDER else 1 - last
                bank_of[product] = last
                place[product] = count[last]
                count[last] += 1
    return bank_of, place, count


BANK, PLACE, PER_STEP = assign_banks()
FRONT_BANKED = [p for p in FRONT_ORDER if p[0] not in NO_BANK]
FIRST = {p: [q for q in FRONT_BANKED if BANK[q] == BANK[p]].index(p) for p in FRONT_BANKED}
FIRST_FRONT = [("LN1", 0), ("LN1", 1), ("Q", 0), ("Q", 1), ("EXP", 0), ("MAP", 0), ("K", 0), ("K", 1), ("EXP", 1),
               ("MAP", 1), ("V", 0), ("V", 1), ("KT", 0), ("KT", 1)]
assert [p for p in FIRST_FRONT if p[0] not in NO_BANK] == FRONT_BANKED
FIRST_COUNT = [len([q for q in FRONT_BANKED if BANK[q] == b]) for b in range(2)]

ATT_MATS = ("q", "k", "v", "o")
NUM_STAGE = 4
NUM_ATT = len(ATT_MATS) + 1
OB_PER_TILE = CH + 1
ROUTER_STEPS = 23


def build(nc, x, w_att, w_up, w_down, w_gate, b_qk, b_vo, b_up, b_down, ident_in, causal_in, own_block_in, rank_in,
          out):
    with ExitStack() as ctx:
        def sb(name, shape, dtype=F32):
            return ctx.enter_context(nc.sbuf_tensor(name, shape, dtype))

        def sem(name):
            return ctx.enter_context(nc.semaphore(name))

        att_hi = [sb(f"w{m}_hi", [P, KC, D], F32R) for m in ATT_MATS]
        att_lo = [sb(f"w{m}_lo", [P, KC, D], F32R) for m in ATT_MATS]
        up_hi = sb("up_hi", [P, NE + 1, KC, HID], F32R)
        up_lo = sb("up_lo", [P, NE + 1, KC, HID], F32R)
        down_hi = sb("down_hi", [P, NE + 1, KC, D], F32R)
        down_lo = sb("down_lo", [P, NE + 1, KC, D], F32R)
        gate_hi = sb("gate_hi", [P, KC, P], F32R)
        gate_lo = sb("gate_lo", [P, KC, P], F32R)
        bdown_hi = sb("bdown_hi", [P, D], F32R)
        bdown_lo = sb("bdown_lo", [P, D], F32R)
        stages = sb("stages", [P, 2, KC * D])
        stage = [stages[:, i, :] for i in range(2)]
        ident = sb("ident_sb", [P, P])
        causal = sb("causal_sb", [P, P])
        rank = sb("rank_sb", [P, CH, NE])
        bqk = sb("bqk", [P, 2 * KC])
        bqk_minus = sb("bqk_minus", [P, 2 * KC])
        bvo = sb("bvo", [P, 2, D])
        bup = sb("bup", [P, (NE + 1) * KC])
        minus_half = sb("minus_half", [P, CH])
        x_in = sb("x_in", [P, 2, CH, D])
        x2 = sb("x2", [P, 2, CH, D])
        xn_q = sb("xn_q", [P, CH * D])
        xn = xn_q[:, :].rearrange("p (c d) -> p c d", c=CH)
        q_map = xn_q[:, :].rearrange("p (k n) -> p k n", k=KC)
        xT_hi = sb("xT_hi", [P, KC, TOK], F32R)
        xT_lo = sb("xT_lo", [P, KC, TOK], F32R)
        q_diag = sb("q_diag", [P, 2, H, P])
        k_map = sb("k_map", [P, KC, TOK])[:, :, :]
        k_tok = sb("k_tok", [P, CH, D])
        v_slot = sb("v_slot", [P, CH, H, SLOT])
        work = sb("work", [P, 2, TOK])
        above = {"Q": k_tok[:, :, :].rearrange("p (k j) d -> p k (j d)", k=KC), "K": work[:, :, :]}
        state = sb("state", [P, 2, H * VW])
        own_state = sb("own_state", [P, H * VW])
        own_block = sb("own_block", [P, HH])
        carry = sb("carry", [P, 2, H, VW])
        o_slot = sb("o_slot", [P, TOK])
        den = sb("den", [P, H])
        rden = sb("rden", [P, H])
        o_sum = sb("o_sum", [P, H, VW])
        o_tok = sb("o_tok", [P, D])
        oT_hi = sb("oT_hi", [P, KC, P], F32R)
        oT_lo = sb("oT_lo", [P, KC, P], F32R)
        x2n = sb("x2n", [P, D])
        x2T_hi = sb("x2T_hi", [P, 2, KC, TOK], F32R)
        x2T_lo = sb("x2T_lo", [P, 2, KC, TOK], F32R)
        stats1, stats = sb("stats1", [P, CH, 6]), sb("stats", [P, CH, 6])
        mv1, mv = sb("mv1", [P, CH, 2]), sb("mv", [P, CH, 2])
        var1, var = sb("var1", [P, CH]), sb("var", [P, CH])
        rstd1, rstd = sb("rstd1", [P, CH]), sb("rstd", [P, CH])
        r_e = sb("r_e", [P, CH, NE])
        r_p = sb("r_p", [P, CH, NE])
        r_a = sb("r_a", [P, CH, NE])
        r_b = sb("r_b", [P, CH, NE])
        r_first = sb("r_first", [P, CH, NE])
        r_rest = sb("r_rest", [P, CH, NE])
        r_s = sb("r_s", [P, 8, CH])
        shares = sb("shares", [P, CH, NE])
        comb = sb("comb", [P, CH, SLOT])
        combT = sb("combT", [P, TOK], F32R)
        h = stages[:, :, :].rearrange("p i (k n) -> p (i k) n", n=TOK)
        assert 2 * KC * D == KC * TOK
        h_hi = [sb(f"h_hi{i}", [P, KC, TOK], F32R) for i in range(2)]
        h_lo = sb("h_lo", [P, KC, TOK], F32R)

        ab = [ctx.enter_context(nc.psum_tensor(f"ab{i}", [P, TOK], F32)) for i in range(2)]
        ob = ctx.enter_context(nc.psum_tensor("ob", [P, TOK], F32))
        cb = ctx.enter_context(nc.psum_tensor("cb", [P, TOK], F32))
        zb = [ctx.enter_context(nc.psum_tensor(f"zb{i}", [P, TOK], F32)) for i in range(KC)]
        yb = [ctx.enter_context(nc.psum_tensor(f"yb{i}", [P, TOK], F32)) for i in range(KC)]

        ident_loaded, bias_loaded, const_loaded = sem("ident_loaded"), sem("bias_loaded"), sem("const_loaded")
        stage_loaded = [sem(f"stage_loaded{i}") for i in range(6)]
        mat_hi = sem("mat_hi")
        mat_lo = sem("mat_lo")
        half_set, slots_zeroed = sem("half_set"), sem("slots_zeroed")
        zeroed = sem("zeroed")
        slots_set = sem("slots_set")
        small_hi = sem("small_hi")
        small_lo = sem("small_lo")
        x_loaded = sem("x_loaded")
        ln1_stats, ln1_mean, ln1_var = sem("ln1_stats"), sem("ln1_mean"), sem("ln1_var")
        ln1_rstd, xn_ready, x_biased = sem("ln1_rstd"), sem("xn_ready"), sem("x_biased")
        ab_full = [sem(f"ab_full{i}") for i in range(2)]
        ab_free = [sem(f"ab_free{i}") for i in range(2)]
        ob_free = sem("ob_free")
        ob_logits, ob_logitsT = sem("ob_logits"), sem("ob_logitsT")
        xT_hi_ready, oT_hi_ready, x2T_hi_ready = sem("xT_hi_ready"), sem("oT_hi_ready"), sem("x2T_hi_ready")
        below_ready, exp_ready = sem("below_ready"), sem("exp_ready")
        queries_mapped, keys_mapped = sem("queries_mapped"), sem("keys_mapped")
        q_spread = [sem(f"q_spread{i}") for i in range(2)]
        state_ready = sem("state_ready")
        group_done = sem("group_done")
        qs_full = sem("qs_full")
        qs_copied = sem("qs_copied")
        own_state_ready = sem("own_state_ready")
        den_ready, rden_ready, o_tok_ready = sem("den_ready"), sem("rden_ready"), sem("o_tok_ready")
        ln2_stats, ln2_mean, ln2_var = sem("ln2_stats"), sem("ln2_mean"), sem("ln2_var")
        ln2_rstd, x2n_ready = sem("ln2_rstd"), sem("x2n_ready")
        router = sem("router")
        router_exp = sem("router_exp")
        combT_ready = sem("combT_ready")
        z_full = sem("z_full")
        h_ready = sem("h_ready")
        cb_full = sem("cb_full")
        h_hi_ready, h_lo_ready = sem("h_hi_ready"), sem("h_lo_ready")
        h_half_used = sem("h_half_used")
        y_full = sem("y_full")
        y_taken = sem("y_taken")
        shares_ready = sem("shares_ready")
        out_stored = sem("out_stored")

        def f32(ap):
            return ap.bitcast(F32)

        primed = {id(s): n for s, n in ((y_taken, 2), (h_ready, 2), (h_lo_ready, 2), (h_half_used, 1),
                                        (y_full, 1), (combT_ready, 1), (cb_full, 1), (out_stored, 16))}

        def after(s, signals):
            if isinstance(signals, int):
                signals = max(signals, 0)
            return signals + primed.get(id(s), 0)

        def part_from_wait(eng):
            eng.nop(nofuse=True)

        def bank(product):
            return ab[BANK[product]]

        def before(product, t):
            b = BANK[product]
            if product not in FRONT_ORDER:
                left_out = 0
                if isinstance(t, int) and t == NT - 1:
                    left_out = len([q for q in FRONT_BANKED if BANK[q] == b and PLACE[q] < PLACE[product]])
                return FIRST_COUNT[b] + PER_STEP[b] * t + PLACE[product] - left_out
            if isinstance(t, int) and t <= 0:
                return FIRST[product] if t == 0 else -1
            return FIRST_COUNT[b] + PER_STEP[b] * (t - 1) + PLACE[product]

        def at_free(product, t):
            n = before(product, t)
            return max(n, 0) if isinstance(n, int) else n

        def at_full(product, t):
            if isinstance(t, int) and t < 0:
                return 0
            return before(product, t) + 1

        def other_bank(product, earlier):
            return BANK[product] != BANK[earlier]

        def full_sem(product):
            return ab_full[BANK[product]]

        def free_sem(product):
            return ab_free[BANK[product]]

        mats = [(att_hi[i][:, :, :], att_lo[i][:, :, :], w_att[i]) for i in range(3)]
        mats.append((gate_hi[:, :, :], gate_lo[:, :, :], w_gate))
        mats.append((att_hi[3][:, :, :], att_lo[3][:, :, :], w_att[3]))
        assert len(mats) == NUM_ATT
        for e in range(NE + 1):
            mats.append((up_hi[:, e], up_lo[:, e], w_up[e]))
            mats.append((down_hi[:, e], down_lo[:, e], w_down[e]))

        def flat(ap):
            return ap.rearrange("p c d -> p (c d)")

        places = [stage[0], stage[1], flat(x2[:, 1, 0:2, :]), flat(x2[:, 1, 2:4, :]),
                  flat(x2[:, 0, 0:2, :]), flat(x2[:, 0, 2:3, :])]
        down_biases = x2[:, 0, 3, :]

        def stage_index(n):
            return (0, 1, 4, 5, 2)[n] if n < NUM_ATT else (n - NUM_ATT) % NUM_STAGE

        def staged(n):
            width = mats[n][2].shape[2]
            return places[stage_index(n)][:, 0:KC * width].rearrange("p (k n) -> p k n", k=KC)

        def loads_of_stage(n):
            return len([m for m in range(n + 1) if stage_index(m) == stage_index(n)])

        def mats_of_gap(g):
            per = 2
            first = NUM_ATT + per * g
            return range(min(first, len(mats)), min(first + per, len(mats)))

        block = ctx.enter_context(nc.Block())

        @block.sync
        def _(sp):
            x_rows = x.rearrange("(t c p) d -> t p c d", c=CH, p=P)
            out_rows = out.rearrange("(t c p) d -> t p c d", c=CH, p=P)
            consts = [(bvo[:, :, :], b_vo), (causal[:, :], causal_in), (own_block[:, :], own_block_in),
                      (rank[:, :, :], rank_in), (bup[:, :], b_up), (down_biases, b_down)]

            def load_mat(n):
                if n >= NUM_ATT:
                    last = max([m for m in range(n) if stage_index(m) == stage_index(n)], default=-1)
                    sp.wait_ge(mat_lo, last + 1)
                    sp.wait_ge(mat_hi, last + 1)
                sp.dma_start(staged(n), mats[n][2]).then_inc(stage_loaded[stage_index(n)], 16)

            def load_x(t):
                sp.dma_start(x_in[:, t % 2, :, :], x_rows[t]).then_inc(x_loaded, 16)

            def spread_q(t, c):
                if c == 0:
                    sp.wait_ge(queries_mapped, t + 1)
                    sp.wait_ge(zeroed, after(zeroed, 1))
                sp.wait_ge(group_done, after(group_done, NG * CH * t + NG * (c - 1)))
                for i in range(HH):
                    sp.dma_start(q_diag[DH * i:DH * (i + 1), c % 2, :, :].rearrange(
                        "p (k i) n -> p i k n", k=KC)[:, i, :, :],
                        q_map[DH * i:DH * (i + 1), :, P * c:P * (c + 1)]).then_inc(q_spread[c % 2], 16)

            def step(t_core, t_front, t_exp):
                spread_q(t_core, 2)
                spread_q(t_core, 3)
                if t_front is not None:
                    if not (isinstance(t_front, int) and t_front + 1 >= NT):
                        sp.wait_ge(free_sem(("OP", CH - 1)), at_full(("OP", CH - 1), t_core))
                        load_x(t_front + 1)
                    spread_q(t_front, 0)
                    spread_q(t_front, 1)
                if t_exp is not None:
                    store(t_exp)

            def store(t):
                sp.wait_ge(y_taken, after(y_taken, 2 * (NE + 1) * (t + 1)))
                sp.dma_start(out_rows[t], x2[:, t % 2, :, :]).then_inc(out_stored, 16)

            sp.sem_inc(y_taken, 2)
            sp.sem_inc(h_ready, 2)
            sp.sem_inc(h_lo_ready, 2)
            sp.sem_inc(cb_full, 1)
            sp.sem_inc(h_half_used, 1)
            sp.sem_inc(y_full, 1)
            sp.sem_inc(combT_ready, 1)
            sp.sem_inc(out_stored, 16)
            load_x(0)
            sp.dma_start(ident[:, :], ident_in).then_inc(ident_loaded, 16)
            load_mat(0)
            sp.dma_start(bqk[:, :], b_qk).then_inc(bias_loaded, 16)
            load_mat(1)
            load_mat(2)
            for dst, src in consts:
                sp.dma_start(dst, src).then_inc(const_loaded, 16)
            for n in range(3, NUM_ATT):
                load_mat(n)
            sp.wait_ge(ln1_stats, 1)
            load_x(1)
            spread_q(0, 0)
            spread_q(0, 1)
            for n in mats_of_gap(0):
                load_mat(n)
            for g in range(GAPS):
                for n in mats_of_gap(g + 1):
                    load_mat(n)
                if g == 1:
                    spread_q(0, 2)
                if g == 3:
                    spread_q(0, 3)
                if g == 11:
                    sp.wait_ge(free_sem(("OP", CH - 1)), at_full(("OP", CH - 1), 0))
                    load_x(2)
                if g == 17:
                    spread_q(1, 0)
                    spread_q(1, 1)
            with sp.Fori(1, NT - 2) as t:
                step(t, t + 1, t - 1)
            step(NT - 2, NT - 1, NT - 3)
            step(NT - 1, None, NT - 2)
            store(NT - 1)
            sp.wait_ge(out_stored, after(out_stored, 16 * NT))

        @block.gpsimd
        def _(pool):
            def input_rstd(t):
                pool.wait_ge(ln1_var, t + 1)
                pool.tensor_tensor(rstd1[:, :], var1[:, :], minus_half[:, :], ALU.pow).then_inc(ln1_rstd, 1)

            pool.memset(minus_half[:, :], -0.5).then_inc(half_set, 1)
            pool.memset(carry[:, :, :, :], 0.0)
            pool.memset(comb[:, :, :], 0.0)
            pool.memset(v_slot[:, :, :, :], 0.0).then_inc(slots_zeroed, 1)
            pool.wait_ge(half_set, 1)
            input_rstd(0)
            pool.memset(q_diag[:, :, :, :], 0.0)
            pool.memset(f32(combT[:, :]), 0.0).then_inc(zeroed, 1)
            pool.wait_ge(zeroed, 1)

            def split_lo(n):
                pool.wait_ge(mat_hi, n + 1)
                pool.tensor_tensor(mats[n][1], staged(n), f32(mats[n][0]), ALU.subtract).then_inc(mat_lo, 1)

            def bias_input(t):
                pool.wait_ge(xn_ready, t + 1)
                pool.tensor_tensor(x_in[:, t % 2, :, :], x_in[:, t % 2, :, :],
                                   bvo[:, 1:2, :].to_broadcast([P, CH, D]), ALU.add).then_inc(x_biased, 1)

            def hidden_lo(e, t):
                n = (NE + 1) * t + e
                for m in range(KC):
                    pool.wait_ge(h_hi_ready, KC * n + m + 1)
                    if m == 0:
                        pool.wait_ge(h_half_used, after(h_half_used, n))
                    else:
                        pool.wait_ge(y_full, after(y_full, 2 * n))
                    pool.tensor_tensor(h_lo[:, m, :], h[:, m, :], f32(h_hi[e % 2][:, m, :]),
                                      ALU.subtract).then_inc(h_lo_ready, 1)

            def take_blocks(c, t):
                if c == 0:
                    pool.wait_ge(state_ready, t + 1)
                else:
                    pool.wait_ge(free_sem(("U", c - 1)), at_full(("U", c - 1), t))
                pool.wait_ge(qs_full, after(qs_full, CH * t + c))
                pool.tensor_tensor(own_state[:, :].rearrange("p (k h w) -> p k h w", k=KC, h=HH),
                                   state[:, c % 2, :].rearrange("p (k h w) -> p k h w", k=KC, h=HH),
                                   own_block[:, :].unsqueeze(1).unsqueeze(3).to_broadcast([P, KC, HH, VW]),
                                   ALU.mult).then_inc(own_state_ready, 1)

            def step(t_core, t_front, t_exp):
                for g in range(GAPS):
                    if g == 0 and t_core is not None:
                        take_blocks(0, t_core)
                    for name, c in GAP[g]:
                        if name == "U" and c < CH - 1 and t_core is not None:
                            take_blocks(c + 1, t_core)
                        if name == "OP" and t_core is not None:
                            pool.wait_ge(ln2_var, CH * t_core + c + 1)
                            pool.tensor_tensor(rstd[:, c:c + 1], var[:, c:c + 1], minus_half[:, c:c + 1],
                                               ALU.pow).then_inc(ln2_rstd, 1)
                    if t_exp is not None and g > 0 and g % 2 == 0:
                        hidden_lo(g // 2 - 1, t_exp)
                    if g == STATS_AT and t_front is not None:
                        input_rstd(t_front)
                    if g == BEFORE_LN1 + 1 and t_front is not None:
                        bias_input(t_front)
                    if t_exp is None:
                        for n in mats_of_gap(g):
                            split_lo(n)

            pool.wait_ge(const_loaded, 16 * 6)
            bias_input(0)
            pool.wait_ge(mat_lo, NUM_ATT)
            step(0, 1, None)
            with pool.Fori(1, NT - 1) as t:
                step(t, t + 1, t - 1)
            step(NT - 1, None, NT - 2)
            step(None, None, NT - 1)

        @block.tensor
        def _(pe):
            def split_product(dst, w_hi, w_lo, x_hi, x_lo, first, last):
                pe.matmul(dst, w_hi, x_hi, start=first, stop=False)
                pe.matmul(dst, w_hi, x_lo, start=False, stop=False)
                return pe.matmul(dst, w_lo, x_hi, start=False, stop=last)

            def project(name, k, t):
                m = ATT_MATS.index(name.lower())
                pe.wait_ge(free_sem((name, k)), at_free((name, k), t))
                for kc in range(KC):
                    last = split_product(bank((name, k))[:, :], att_hi[m][:, kc, P * k:P * (k + 1)],
                                         att_lo[m][:, kc, P * k:P * (k + 1)], xT_hi[:, kc, :], xT_lo[:, kc, :],
                                         kc == 0, kc == KC - 1)
                last.then_inc(full_sem((name, k)), 1)

            def core(c, half, t):
                groups = (2 * half, 2 * half + 1)
                if half == 0:
                    if c % 2 == 0:
                        pe.wait_ge(q_spread[0], 16 * HH * (2 * t + c // 2 + 1))
                    else:
                        pe.wait_ge(q_spread[1], 16 * HH * (2 * t + c // 2 + 1))
                    pe.wait_ge(keys_mapped, t + 1)
                for g in groups:
                    k = g * HG // HH
                    pe.wait_ge(free_sem(("A", NG * c + g)), at_free(("A", NG * c + g), t))
                    pe.matmul(bank(("A", NG * c + g))[:, :], k_map[:, k, P * c:P * (c + 1)],
                              q_diag[:, c % 2, HG * g:HG * (g + 1), :], start=True, stop=True)\
                        .then_inc(full_sem(("A", NG * c + g)), 1)

            def from_state(c, t):
                pe.wait_ge(own_state_ready, CH * t + c + 1)
                if c == 0:
                    pe.wait_ge(combT_ready, after(combT_ready, t - 1))
                else:
                    pe.wait_ge(qs_copied, CH * t + c)
                for k in range(KC):
                    at = HH * VW * k
                    last = pe.matmul(cb[:, at:at + HH * VW], q_map[:, k, P * c:P * (c + 1)],
                                     own_state[:, at:at + HH * VW], start=True, stop=True)
                last.then_inc(qs_full, 1)

            def outputs(c, half, t):
                if half == 0:
                    pe.wait_ge(ob_free, after(ob_free, OB_PER_TILE * t + c))
                    if c == 0:
                        pe.wait_ge(router, after(router, ROUTER_STEPS * t))
                for g in (2 * half, 2 * half + 1):
                    pe.wait_ge(free_sem(("A", NG * c + g)), at_full(("A", NG * c + g), t))
                    for i in range(HG):
                        last = pe.matmul(ob[SLOT * i:SLOT * (i + 1), P * g:P * (g + 1)],
                                         v_slot[:, c, HG * g + i, :], work[:, g % 2, P * i:P * (i + 1)],
                                         start=g == 0, stop=True, skip_group_check=True)
                    last.then_inc(group_done, 1)

            def attention_product(name, c, t):
                if name in ("EXP", "REXP", "MAP"):
                    return
                if name == "CORE":
                    core(c // 2, c % 2, t)
                    return
                if name == "AV":
                    outputs(c // 2, c % 2, t)
                    return
                if name == "QS":
                    from_state(c, t)
                    return
                if name in ("Q", "K"):
                    if (name, c) == ("Q", 0):
                        if isinstance(t, int) and t == 0:
                            pe.wait_ge(mat_lo, 2)
                            pe.wait_ge(mat_hi, 2)
                        pe.wait_ge(free_sem(("LN1", 1)), at_full(("LN1", 1), t))
                        pe.wait_ge(free_sem(("LN1", 0)), at_full(("LN1", 0), t))
                    project(name, c, t)
                    return
                if name == "LG":
                    pe.wait_ge(free_sem(("X2T", CH - 1)), at_full(("X2T", CH - 1), t))
                    pe.wait_ge(ob_free, OB_PER_TILE * t + CH)
                    for kc in range(KC):
                        last = split_product(ob[:, :], gate_hi[:, kc, :], gate_lo[:, kc, :],
                                             x2T_hi[:, t % 2, kc, :], x2T_lo[:, t % 2, kc, :],
                                             kc == 0, kc == KC - 1)
                    last.then_inc(ob_logits, 1)
                    return
                if name == "LGT":
                    pe.wait_ge(ob_free, OB_PER_TILE * t + CH + 1)
                    part_from_wait(pe)
                    for j in range(CH):
                        last = pe.transpose(ob[:, NE * j:NE * (j + 1)], o_slot[0:NE, P * j:P * (j + 1)],
                                            ident[0:NE, 0:NE])
                    last.then_inc(ob_logitsT, 1)
                    return
                product = (name, c)
                dst = bank(product)
                if name == "LN1":
                    pe.wait_ge(xn_ready, t + 1)
                    pe.wait_ge(free_sem(product), at_free(product, t))
                    for j in range(CH):
                        last = pe.transpose(dst[:, P * j:P * (j + 1)], xn[:, j, P * c:P * (c + 1)], ident[:, :])
                if name == "V":
                    pe.wait_ge(free_sem(product), at_free(product, t))
                    if isinstance(t, int) and t == 0:
                        pe.wait_ge(mat_lo, ATT_MATS.index("v") + 1)
                    for j in range(2):
                        at = P * (2 * c + j)
                        for kc in range(KC):
                            last = split_product(dst[:, D * j:D * (j + 1)], xT_hi[:, kc, at:at + P],
                                                 xT_lo[:, kc, at:at + P], att_hi[2][:, kc, :], att_lo[2][:, kc, :],
                                                 kc == 0, kc == KC - 1)
                if name == "KT":
                    pe.wait_ge(keys_mapped, t + 1)
                    pe.wait_ge(free_sem(product), at_free(product, t))
                    for j in range(2):
                        for k in range(KC):
                            at = P * (2 * c + j)
                            last = pe.transpose(dst[:, D * j + P * k:D * j + P * (k + 1)],
                                                k_map[:, k, at:at + P], ident[:, :])
                if name == "U":
                    keys = ("KT", c // 2)
                    assert not other_bank(keys, ("V", c // 2))
                    if other_bank(product, keys):
                        pe.wait_ge(free_sem(keys), at_full(keys, t))
                    pe.wait_ge(free_sem(product), at_free(product, t))
                    for k in range(KC):
                        last = pe.matmul(dst[:, HH * VW * k:HH * VW * (k + 1)], k_tok[:, c, P * k:P * (k + 1)],
                                         v_slot[:, c, HH * k:HH * (k + 1), 0:VW], start=True, stop=True)
                if name == "T":
                    pe.wait_ge(ob_free, OB_PER_TILE * t + c + 1)
                    pe.wait_ge(free_sem(product), at_free(product, t))
                    for g in range(NG):
                        last = pe.transpose(dst[:, P * g:P * (g + 1)], o_slot[:, P * g:P * (g + 1)], ident[:, :])
                if name == "OT":
                    pe.wait_ge(o_tok_ready, CH * t + c + 1)
                    pe.wait_ge(free_sem(product), at_free(product, t))
                    for k in range(KC):
                        last = pe.transpose(dst[:, P * k:P * (k + 1)], o_tok[:, P * k:P * (k + 1)], ident[:, :])
                if name == "OP":
                    if c == 0 and isinstance(t, int) and t == 0:
                        pe.wait_ge(mat_lo, NUM_ATT)
                    if other_bank(product, ("OT", c)):
                        pe.wait_ge(free_sem(("OT", c)), at_full(("OT", c), t))
                    pe.wait_ge(free_sem(product), at_free(product, t))
                    for kc in range(KC):
                        last = split_product(dst[:, 0:D], oT_hi[:, kc, :], oT_lo[:, kc, :],
                                             att_hi[3][:, kc, :], att_lo[3][:, kc, :], kc == 0, kc == KC - 1)
                if name == "X2T":
                    pe.wait_ge(x2n_ready, CH * t + c + 1)
                    pe.wait_ge(free_sem(product), at_free(product, t))
                    for k in range(KC):
                        last = pe.transpose(dst[:, P * k:P * (k + 1)], x2n[:, P * k:P * (k + 1)], ident[:, :])
                last.then_inc(full_sem(product), 1)

            def attention_gap(g, t_core, t_front):
                for name, c in GAP[g]:
                    t = t_front if (name, c) in FRONT_ORDER else t_core
                    if t is not None:
                        attention_product(name, c, t)

            def up(e, t):
                for m in range(KC):
                    pe.wait_ge(h_ready, after(h_ready, KC * ((NE + 1) * t + e - 1) + m + 1))
                    for kc in range(KC):
                        last = split_product(zb[m][:, :], up_hi[:, e, kc, P * m:P * (m + 1)],
                                             up_lo[:, e, kc, P * m:P * (m + 1)], x2T_hi[:, t % 2, kc, :],
                                             x2T_lo[:, t % 2, kc, :], kc == 0, kc == KC - 1)
                    last.then_inc(z_full, 1)

            def share_transpose(t):
                pe.wait_ge(router, ROUTER_STEPS * (t + 1))
                if isinstance(t, int) and t == NT - 1:
                    pe.wait_ge(qs_copied, CH * NT)
                else:
                    pe.wait_ge(qs_copied, CH * (t + 2))
                for j in range(CH):
                    last = pe.transpose(cb[0:SLOT, P * j:P * (j + 1)], comb[:, j, :], ident[:, :])
                last.then_inc(cb_full, 1)

            def down(e, t):
                n = (NE + 1) * t + e
                if e == NE:
                    pe.wait_ge(combT_ready, after(combT_ready, t + 1))
                    for c in range(CH):
                        dst = yb[c // 2][:, D * (c % 2):D * (c % 2 + 1)]
                        if c % 2 == 0:
                            pe.wait_ge(y_taken, after(y_taken, 2 * (n - 1) + c // 2 + 1))
                        shares = combT[:, P * c:P * (c + 1)]
                        pe.matmul(dst, shares, bdown_hi[:, :], start=c % 2 == 0, stop=False, skip_group_check=True)
                        pe.matmul(dst, shares, bdown_lo[:, :], start=False, stop=False, skip_group_check=True)
                for k in range(KC):
                    pe.wait_ge(h_lo_ready, after(h_lo_ready, KC * n + k + 1))
                    for c in range(CH):
                        dst = yb[c // 2][:, D * (c % 2):D * (c % 2 + 1)]
                        first = e < NE and k == 0 and c % 2 == 0
                        if first:
                            pe.wait_ge(y_taken, after(y_taken, 2 * (n - 1) + c // 2 + 1))
                        hi, lo = h_hi[e % 2][:, k, P * c:P * (c + 1)], h_lo[:, k, P * c:P * (c + 1)]
                        pe.matmul(dst, hi, down_hi[:, e, k, :], start=first, stop=False, skip_group_check=True)
                        pe.matmul(dst, hi, down_lo[:, e, k, :], start=False, stop=False, skip_group_check=True)
                        last = pe.matmul(dst, lo, down_hi[:, e, k, :], start=False, stop=k == KC - 1,
                                         skip_group_check=True)
                        if k == KC - 1 and c % 2 == 1:
                            last.then_inc(y_full, 1)
                    if k == 0:
                        last.then_inc(h_half_used, 1)

            def step(t_core, t_front, t_exp):
                for g in range(GAPS):
                    attention_gap(g, t_core, t_front)
                    if t_exp is not None:
                        e = g // 2
                        if e <= NE and g % 2 == 0:
                            up(e, t_exp)
                            if g == SHARES_AT:
                                share_transpose(t_exp)
                        if e > 0 and g % 2 == 1:
                            down(e - 1, t_exp)

            pe.wait_ge(ident_loaded, 16)
            for name, c in FIRST_FRONT:
                attention_product(name, c, 0)
            step(0, 1, None)
            pe.wait_ge(mat_lo, len(mats))
            pe.wait_ge(small_lo, 1)
            pe.wait_ge(slots_set, 1)
            pe.wait_ge(small_hi, 1)
            with pe.Fori(1, NT - 1) as t:
                step(t, t + 1, t - 1)
            step(NT - 1, None, NT - 2)
            step(None, None, NT - 1)

        @block.scalar
        def _(act):
            def split_hi(n):
                act.wait_ge(stage_loaded[stage_index(n)], 16 * loads_of_stage(n))
                act.activation(mats[n][0], staged(n), ACT.Copy).then_inc(mat_hi, 1)

            def attention_product(name, c, t):
                product = (name, c)
                if name == "LN1":
                    act.wait_ge(full_sem(product), at_full(product, t))
                    act.activation(xT_hi[:, c, :], bank(product)[:, :], ACT.Copy).then_inc(xT_hi_ready, 1)
                if name in ("Q", "K"):
                    n = KC * (name == "K") + c
                    act.wait_ge(full_sem(product), at_full(product, t))
                    below = (q_map if name == "Q" else k_map)[:, c, :]
                    act.activation(below, bank(product)[:, :], ACT.Relu, scale=-1.0,
                                   bias=bqk_minus[:, n:n + 1]).then_inc(below_ready, 1)
                    act.activation(above[name][:, c, :], bank(product)[:, :], ACT.Relu,
                                   bias=bqk[:, n:n + 1]).then_inc(free_sem(product), 1)
                if name == "EXP":
                    z = (q_map, k_map)[c]
                    act.wait_ge(below_ready, 2 * KC * t + KC * (c + 1))
                    act.activation(z, z, ACT.Exp, scale=-1.0).then_inc(exp_ready, 1)
                if name == "QS":
                    act.wait_ge(qs_full, CH * t + c + 1)
                    act.wait_ge(o_tok_ready, after(o_tok_ready, CH * t + c))
                    act.activation(o_sum[:, :, :], cb[:, 0:H * VW].rearrange("p (h w) -> p h w", h=H),
                                   ACT.Copy).then_inc(qs_copied, 1)
                if name == "KT":
                    act.wait_ge(full_sem(product), at_full(product, t))
                    if c == 0:
                        if other_bank(product, ("U", CH - 1)):
                            act.wait_ge(full_sem(("U", CH - 1)), at_full(("U", CH - 1), t - 1))
                    act.activation(k_tok[:, 2 * c:2 * c + 2, :], bank(product)[:, :].rearrange(
                        "p (j d) -> p j d", j=2), ACT.Copy).then_inc(free_sem(product), 1)
                if name == "AV" and c % 2 == 1:
                    act.wait_ge(group_done, NG * (CH * t + c // 2 + 1))
                    if c // 2 > 0:
                        act.wait_ge(full_sem(("T", c // 2 - 1)), at_full(("T", c // 2 - 1), t))
                    else:
                        act.wait_ge(ob_logitsT, after(ob_logitsT, t))
                    act.activation(o_slot[:, :], ob[:, :], ACT.Copy).then_inc(ob_free, 1)
                if name == "OT":
                    act.wait_ge(full_sem(product), at_full(product, t))
                    if c > 0 and other_bank(product, ("OP", c - 1)):
                        act.wait_ge(full_sem(("OP", c - 1)), at_full(("OP", c - 1), t))
                    act.activation(oT_hi[:, :, :], bank(product)[:, 0:D].rearrange("p (k n) -> p k n", k=KC),
                                   ACT.Copy).then_inc(oT_hi_ready, 1)
                if name == "X2T":
                    act.wait_ge(full_sem(product), at_full(product, t))
                    act.activation(x2T_hi[:, t % 2, :, P * c:P * (c + 1)],
                                   bank(product)[:, 0:D].rearrange("p (k n) -> p k n", k=KC),
                                   ACT.Copy).then_inc(x2T_hi_ready, 1)
                if name == "LG":
                    act.wait_ge(ob_logits, t + 1)
                    act.wait_ge(full_sem(("T", CH - 1)), at_full(("T", CH - 1), t))
                    act.activation(o_slot[0:NE, :], ob[0:NE, :], ACT.Copy).then_inc(ob_free, 1)
                if name == "REXP":
                    act.wait_ge(router, after(router, ROUTER_STEPS * t + 2))
                    act.activation(r_e[:, :, :], r_a[:, :, :], ACT.Exp).then_inc(router_exp, 1)

            def attention_gap(g, t_core, t_front):
                for name, c in GAP[g]:
                    t = t_front if (name, c) in FRONT_ORDER else t_core
                    if t is not None:
                        attention_product(name, c, t)

            def hidden(e, t):
                n = (NE + 1) * t + e
                for m in range(KC):
                    act.wait_ge(z_full, KC * n + m + 1)
                    act.wait_ge(h_lo_ready, after(h_lo_ready, KC * (n - 1) + m + 1))
                    act.activation(h[:, m, :], zb[m][:, :], ACT.Silu,
                                   bias=bup[:, KC * e + m:KC * e + m + 1]).then_inc(h_ready, 1)

            def hidden_hi(e, t):
                n = (NE + 1) * t + e
                last = n - 1 if e == 0 else n - 2
                for m in range(KC):
                    act.wait_ge(h_ready, after(h_ready, KC * n + m + 1))
                    if m == 0:
                        act.wait_ge(h_half_used, after(h_half_used, last + 1))
                    else:
                        act.wait_ge(y_full, after(y_full, 2 * (last + 1)))
                    act.activation(h_hi[e % 2][:, m, :], h[:, m, :], ACT.Copy).then_inc(h_hi_ready, 1)

            def step(t_core, t_front, t_exp):
                for g in range(GAPS):
                    attention_gap(g, t_core, t_front)
                    if t_exp is None:
                        for n in mats_of_gap(g):
                            split_hi(n)
                        continue
                    e = g // 2
                    if e <= NE and g % 2 == 1:
                        hidden_hi(e, t_exp)
                    if e <= NE and g % 2 == 0:
                        hidden(e, t_exp)
                        if g == SHARES_AT:
                            act.wait_ge(cb_full, after(cb_full, t_exp + 1))
                            act.activation(combT[0:SLOT, :], cb[0:SLOT, :], ACT.Copy).then_inc(combT_ready, 1)

            split_hi(0)
            split_hi(1)
            act.wait_ge(slots_set, 2)
            for name, c in FIRST_FRONT:
                attention_product(name, c, 0)
                if (name, c) == ("LN1", 1):
                    for n in range(2, NUM_ATT):
                        split_hi(n)
            act.wait_ge(const_loaded, 16 * 6)
            act.activation(bdown_hi[:, :], down_biases, ACT.Copy).then_inc(small_hi, 1)
            step(0, 1, None)
            act.wait_ge(small_lo, 1)
            act.wait_ge(zeroed, 1)
            act.wait_ge(mat_lo, len(mats))
            with act.Fori(1, NT - 1) as t:
                step(t, t + 1, t - 1)
            step(NT - 1, None, NT - 2)
            step(None, None, NT - 1)

        @block.vector
        def _(dve):
            def per_token(ap, n):
                return ap.unsqueeze(2).to_broadcast([P, CH, n])

            def input_stats(t):
                dve.wait_ge(x_loaded, 16 * (t + 1))
                dve.wait_ge(ln1_rstd, after(ln1_rstd, t))
                for c in range(CH):
                    last = dve.bn_stats(stats1[:, c, :], x_in[:, t % 2, c, :])
                last.then_inc(ln1_stats, 1)
                dve.wait_ge(ln1_stats, t + 1)
                part_from_wait(dve)
                for c in range(CH):
                    last = dve.bn_aggr(mv1[:, c, :], stats1[:, c, :])
                last.then_inc(ln1_mean, 1)
                dve.wait_ge(ln1_mean, t + 1)
                dve.tensor_scalar(var1[:, :], mv1[:, :, 1], EPS_LN, None, ALU.add).then_inc(ln1_var, 1)

            def norm_input(t):
                dve.wait_ge(ln1_rstd, t + 1)
                dve.wait_ge(q_spread[0], after(q_spread[0], 32 * HH * t))
                dve.wait_ge(q_spread[1], after(q_spread[1], 32 * HH * t))
                for c in range(CH):
                    last = dve.tensor_scalar(xn[:, c, :], x_in[:, t % 2, c, :], mv1[:, c, 0:1], rstd1[:, c:c + 1],
                                             ALU.subtract, ALU.mult)
                last.then_inc(xn_ready, 1)

            def attention_product(name, c, t):
                product = (name, c)
                if name == "LN1":
                    dve.wait_ge(xT_hi_ready, KC * t + c + 1)
                    dve.tensor_tensor(xT_lo[:, c, :], bank(product)[:, :], f32(xT_hi[:, c, :]),
                                      ALU.subtract).then_inc(free_sem(product), 1)
                if name == "MAP":
                    z, relu, done = ((q_map, above["Q"], queries_mapped), (k_map, above["K"], keys_mapped))[c]
                    dve.wait_ge(exp_ready, 2 * t + c + 1)
                    dve.tensor_tensor(z, z, relu, ALU.add).then_inc(done, 1)
                if name == "V":
                    dve.wait_ge(full_sem(product), at_full(product, t))
                    if c == 0:
                        dve.wait_ge(group_done, after(group_done, NG * CH * t))
                    dve.tensor_tensor(v_slot[:, 2 * c:2 * c + 2, :, 0:DH],
                                      bank(product)[:, :].rearrange("p (j h d) -> p j h d", j=2, h=H),
                                      bvo[:, 0:1, :].rearrange("p j (h d) -> p j h d", h=H).to_broadcast(
                                          [P, 2, H, DH]), ALU.add).then_inc(free_sem(product), 1)
                if name == "U":
                    if c == 0:
                        dve.wait_ge(state_ready, t + 1)
                    else:
                        dve.wait_ge(free_sem(("U", c - 1)), at_full(("U", c - 1), t))
                        dve.wait_ge(own_state_ready, CH * t + c)
                    dve.wait_ge(full_sem(product), at_full(product, t))
                    dst = state[:, (c + 1) % 2, :] if c < CH - 1 else carry[:, 1, :, :].rearrange("p h w -> p (h w)")
                    dve.tensor_tensor(dst, bank(product)[:, 0:H * VW], state[:, c % 2, :],
                                      ALU.add).then_inc(free_sem(product), 1)
                if name == "CORE":
                    for i in range(2):
                        g = 2 * (c % 2) + i
                        n = NG * (c // 2) + g
                        dve.wait_ge(full_sem(("A", n)), at_full(("A", n), t))
                        dve.wait_ge(group_done, after(group_done, NG * CH * t + n - 1))
                        dve.tensor_tensor(work[:, g % 2, :].rearrange("p (i n) -> p i n", i=HG),
                                          bank(("A", n))[:, :].rearrange("p (i n) -> p i n", i=HG),
                                          causal[:, :].unsqueeze(1).to_broadcast([P, HG, P]),
                                          ALU.mult).then_inc(free_sem(("A", n)), 1)
                if name == "T":
                    n = CH * t + c + 1
                    dve.wait_ge(full_sem(product), at_full(product, t))
                    dve.wait_ge(qs_copied, n)
                    dve.tensor_tensor(o_sum[:, :, :], bank(product)[:, :].rearrange(
                        "p (h s) -> p h s", h=H)[:, :, 0:VW], o_sum[:, :, :], ALU.add).then_inc(free_sem(product), 1)
                    dve.wait_ge(free_sem(product), at_full(product, t))
                    dve.tensor_scalar(den[:, :], o_sum[:, :, DH], EPS_DEN, None, ALU.max).then_inc(den_ready, 1)
                    dve.wait_ge(den_ready, n)
                    dve.reciprocal(rden[:, :], den[:, :]).then_inc(rden_ready, 1)
                    dve.wait_ge(rden_ready, n)
                    dve.tensor_tensor(o_tok[:, :].rearrange("p (h d) -> p h d", h=H), o_sum[:, :, 0:DH],
                                      rden[:, :].unsqueeze(2).to_broadcast([P, H, DH]),
                                      ALU.mult).then_inc(o_tok_ready, 1)
                if name == "OT":
                    dve.wait_ge(oT_hi_ready, CH * t + c + 1)
                    dve.tensor_tensor(oT_lo[:, :, :], bank(product)[:, 0:D].rearrange("p (k n) -> p k n", k=KC),
                                      f32(oT_hi[:, :, :]), ALU.subtract).then_inc(free_sem(product), 1)
                if name == "OP":
                    n = CH * t + c + 1
                    dve.wait_ge(full_sem(product), at_full(product, t))
                    if c == 0:
                        dve.wait_ge(x_biased, t + 1)
                        dve.wait_ge(out_stored, after(out_stored, 16 * (t - 1)))
                    dve.tensor_tensor(x2[:, t % 2, c, :], bank(product)[:, 0:D], x_in[:, t % 2, c, :],
                                      ALU.add).then_inc(free_sem(product), 1)
                    dve.wait_ge(free_sem(product), at_full(product, t))
                    part_from_wait(dve)
                    dve.bn_stats(stats[:, c, :], x2[:, t % 2, c, :]).then_inc(ln2_stats, 1)
                    dve.wait_ge(ln2_stats, after(ln2_stats, n))
                    part_from_wait(dve)
                    dve.bn_aggr(mv[:, c, :], stats[:, c, :]).then_inc(ln2_mean, 1)
                    dve.wait_ge(ln2_mean, after(ln2_mean, n))
                    dve.tensor_scalar(var[:, c:c + 1], mv[:, c, 1:2], EPS_LN, None, ALU.add).then_inc(ln2_var, 1)
                if name == "X2T":
                    dve.wait_ge(x2T_hi_ready, CH * t + c + 1)
                    dve.tensor_tensor(x2T_lo[:, t % 2, :, P * c:P * (c + 1)],
                                      bank(product)[:, 0:D].rearrange("p (k n) -> p k n", k=KC),
                                      f32(x2T_hi[:, t % 2, :, P * c:P * (c + 1)]),
                                      ALU.subtract).then_inc(free_sem(product), 1)
                if name == "LGT":
                    dve.wait_ge(ob_logitsT, t + 1)
                    route(0, t)

            def take_state(t):
                dve.wait_ge(free_sem(("U", CH - 1)), at_full(("U", CH - 1), t - 1))
                dve.wait_ge(own_state_ready, after(own_state_ready, CH * t))
                dve.tensor_copy(state[:, 0, :], carry[:, (t % TPB + TPB - 1) // TPB, :, :].rearrange(
                    "p h w -> p (h w)")).then_inc(state_ready, 1)

            def norm_residual(c, t):
                n = CH * t + c + 1
                dve.wait_ge(ln2_rstd, after(ln2_rstd, n))
                if c > 0:
                    dve.wait_ge(full_sem(("X2T", c - 1)), at_full(("X2T", c - 1), t))
                dve.tensor_scalar(x2n[:, :], x2[:, t % 2, c, :], mv[:, c, 0:1], rstd[:, c:c + 1],
                                  ALU.subtract, ALU.mult).then_inc(x2n_ready, 1)

            def route(part, t):
                done = [0, 2, 8, 16][part:part + 1]

                def then(ins):
                    done[0] += 1
                    ins.then_inc(router, 1)
                    dve.wait_ge(router, after(router, ROUTER_STEPS * t + done[0]))

                lgT = ob[:, 0:CH * NE].rearrange("p (c e) -> p c e", c=CH)
                m, s, rs, p1, at1, p2, at2, tot = (r_s[:, i, :] for i in range(8))
                if part == 0:
                    then(dve.tensor_reduce(m, lgT, AX_X, ALU.max))
                    then(dve.tensor_tensor(r_a[:, :, :], lgT, per_token(m, NE), ALU.subtract))
                if part == 1:
                    dve.wait_ge(router_exp, t + 1)
                    then(dve.tensor_reduce(s, r_e[:, :, :], AX_X, ALU.add))
                    then(dve.reciprocal(rs, s))
                    then(dve.tensor_tensor(r_p[:, :, :], r_e[:, :, :], per_token(rs, NE), ALU.mult))
                    then(dve.tensor_reduce(p1, r_p[:, :, :], AX_X, ALU.max))
                    then(dve.tensor_tensor(r_b[:, :, :], r_p[:, :, :], per_token(p1, NE), ALU.is_equal))
                    then(dve.tensor_tensor(r_b[:, :, :], r_b[:, :, :], rank[:, :, :], ALU.mult))
                if part == 2:
                    then(dve.tensor_reduce(at1, r_b[:, :, :], AX_X, ALU.max))
                    then(dve.tensor_tensor(r_first[:, :, :], r_b[:, :, :], per_token(at1, NE), ALU.is_equal))
                    then(dve.scalar_tensor_tensor(out=r_rest[:, :, :], in0=r_first[:, :, :], scalar=-2.0,
                                                  in1=r_p[:, :, :], op0=ALU.mult, op1=ALU.add))
                    then(dve.tensor_reduce(p2, r_rest[:, :, :], AX_X, ALU.max))
                    then(dve.tensor_tensor(r_b[:, :, :], r_rest[:, :, :], per_token(p2, NE), ALU.is_equal))
                    then(dve.tensor_tensor(r_b[:, :, :], r_b[:, :, :], rank[:, :, :], ALU.mult))
                    then(dve.tensor_reduce(at2, r_b[:, :, :], AX_X, ALU.max))
                    then(dve.tensor_tensor(r_b[:, :, :], r_b[:, :, :], per_token(at2, NE), ALU.is_equal))
                if part == 3:
                    then(dve.tensor_tensor(r_b[:, :, :], r_b[:, :, :], r_first[:, :, :], ALU.add))
                    then(dve.tensor_tensor(r_b[:, :, :], r_b[:, :, :], r_p[:, :, :], ALU.mult))
                    then(dve.scalar_tensor_tensor(out=tot, in0=p1, scalar=1e-20, in1=p2, op0=ALU.add, op1=ALU.add))
                    then(dve.reciprocal(rs, tot))
                    then(dve.tensor_tensor(r_b[:, :, :], r_b[:, :, :], per_token(rs, NE), ALU.mult))
                    dve.wait_ge(cb_full, after(cb_full, t))
                    then(dve.tensor_copy(comb[:, :, 0:NE].bitcast(F32R), r_b[:, :, :]))
                    then(dve.tensor_tensor(comb[:, :, NE:2 * NE].bitcast(F32R), r_b[:, :, :], comb[:, :, 0:NE],
                                           ALU.subtract))
                    assert done[0] == ROUTER_STEPS

            def attention_gap(g, t_core, t_front):
                if g == 0 and t_core is not None:
                    take_state(t_core)
                for name, c in GAP[g]:
                    t = t_front if (name, c) in FRONT_ORDER else t_core
                    if t is not None:
                        attention_product(name, c, t)
                if g + 1 < GAPS and t_core is not None:
                    for name, c in GAP[g + 1]:
                        if name == "X2T":
                            norm_residual(c, t_core)

            def take_shares(t):
                dve.wait_ge(router, ROUTER_STEPS * (t + 1))
                dve.tensor_copy(shares[:, :, :], r_b[:, :, :]).then_inc(shares_ready, 1)

            def add_expert(e, t):
                for c in range(CH):
                    if c % 2 == 0:
                        dve.wait_ge(y_full, after(y_full, 2 * ((NE + 1) * t + e) + c // 2 + 1))
                    if c == 0 and e == 0:
                        dve.wait_ge(shares_ready, t + 1)
                    at = x2[:, t % 2, c, :]
                    ins = dve.scalar_tensor_tensor(out=at, in0=yb[c // 2][:, D * (c % 2):D * (c % 2 + 1)],
                                                   scalar=shares[:, c, e:e + 1], in1=at, op0=ALU.mult, op1=ALU.add)
                    if c % 2 == 1:
                        ins.then_inc(y_taken, 1)

            def add_shared(t):
                for j in range(2):
                    dve.wait_ge(y_full, after(y_full, 2 * ((NE + 1) * t + NE) + j + 1))
                    at = x2[:, t % 2, 2 * j:2 * j + 2, :]
                    dve.tensor_tensor(at, yb[j][:, :].rearrange("p (j d) -> p j d", j=2), at,
                                      ALU.add).then_inc(y_taken, 1)

            def step(t_core, t_front, t_exp):
                for g in range(GAPS):
                    experts_first = g >= 18
                    if not experts_first:
                        attention_gap(g, t_core, t_front)
                    if t_exp is not None and g == 0:
                        take_shares(t_exp)
                    if t_exp is not None and g >= 4 and g % 2 == 0:
                        add_expert(g // 2 - 2, t_exp)
                    if experts_first:
                        attention_gap(g, t_core, t_front)
                    if g == STATS_AT and t_front is not None:
                        input_stats(t_front)
                    if g == BEFORE_LN1 and t_front is not None:
                        norm_input(t_front)
                    if g in ROUTE_AT and t_core is not None:
                        route(1 + ROUTE_AT.index(g), t_core)
                if t_exp is not None:
                    add_shared(t_exp)

            def split_lo(n):
                dve.wait_ge(mat_hi, n + 1)
                dve.tensor_tensor(mats[n][1], staged(n), f32(mats[n][0]), ALU.subtract).then_inc(mat_lo, 1)

            input_stats(0)
            dve.wait_ge(slots_zeroed, 1)
            dve.memset(v_slot[:, :, :, DH:VW], 1.0)
            dve.memset(comb[:, :, 2 * NE:2 * NE + 1], 1.0).then_inc(slots_set, 1)
            norm_input(0)
            dve.wait_ge(bias_loaded, 16)
            dve.tensor_scalar(bqk_minus[:, :], bqk[:, :], -1.0, None, ALU.mult).then_inc(slots_set, 1)
            split_lo(0)
            split_lo(1)
            for name, c in FIRST_FRONT:
                attention_product(name, c, 0)
                if (name, c) == ("LN1", 1):
                    split_lo(2)
                if (name, c) == ("MAP", 0):
                    for n in range(3, NUM_ATT):
                        split_lo(n)
                    dve.wait_ge(const_loaded, 16 * 6)
            dve.wait_ge(zeroed, 1)
            dve.wait_ge(small_hi, 1)
            dve.tensor_tensor(bdown_lo[:, :], down_biases, f32(bdown_hi[:, :]), ALU.subtract).then_inc(small_lo, 1)
            step(0, 1, None)
            with dve.Fori(1, NT - 1) as t:
                step(t, t + 1, t - 1)
            step(NT - 1, None, NT - 2)
            step(None, None, NT - 1)


def kernel(**inputs):
    import numpy as np
    import concourse.bacc as bacc
    from concourse.bass_utils import run_bass_kernel_spmd as run

    a = {k: np.ascontiguousarray(v) for k, v in inputs.items()}

    def by_rows(w):
        w = w.reshape(w.shape[:-2] + (KC, P, w.shape[-1]))
        return np.ascontiguousarray(np.swapaxes(w, -3, -2))

    gate = np.zeros((D, P), np.float32)
    gate[:, :NE] = a["L0_ffn_gate_w"].T
    b_down = np.zeros((P, D), np.float32)
    b_down[0:NE] = a["L0_ffn_down_b"]
    b_down[NE:2 * NE] = a["L0_ffn_down_b"]
    b_down[2 * NE] = a["L0_ffn_sh_down_b"]
    b_up = np.concatenate([a["L0_ffn_up_b"], a["L0_ffn_sh_up_b"][None]])
    arrays = {
        "in_x": a["L0_attn_x"].reshape(B * T, D),
        "in_w_att": by_rows(np.stack([a[f"L0_attn_W{m}"].T for m in ATT_MATS])),
        "in_w_up": by_rows(np.concatenate([a["L0_ffn_up_w"], a["L0_ffn_sh_up_w"][None]])),
        "in_w_down": by_rows(np.concatenate([a["L0_ffn_down_w"], a["L0_ffn_sh_down_w"][None]])),
        "in_w_gate": by_rows(gate),
        "in_b_qk": np.ascontiguousarray(np.concatenate([a["L0_attn_bq"].reshape(KC, P),
                                                        a["L0_attn_bk"].reshape(KC, P)]).T),
        "in_b_vo": np.ascontiguousarray(np.broadcast_to(np.stack([a["L0_attn_bv"], a["L0_attn_bo"]]), (P, 2, D))),
        "in_b_up": np.ascontiguousarray(b_up.reshape((NE + 1) * KC, P).T),
        "in_b_down": b_down,
        "in_ident": np.eye(P, dtype=np.float32),
        "in_causal": np.triu(np.ones((P, P), np.float32)),
        "in_own_block": np.repeat(np.eye(HH, dtype=np.float32), DH, axis=0),
        "in_rank": np.ascontiguousarray(np.broadcast_to(np.arange(NE, 0, -1, dtype=np.float32), (P, CH, NE))),
    }
    nc = bacc.Bacc("TRN2", target_bir_lowering=False, num_devices=1)
    args = [nc.dram_tensor(name, v.shape, mybir.dt.from_np(v.dtype), kind="ExternalInput").ap()
            for name, v in arrays.items()]
    out = nc.dram_tensor("out", (B * T, D), F32, kind="ExternalOutput").ap()
    build(nc, *args[:5], args[5], args[6], args[7], args[8], *args[9:], out)
    r = run(nc, [arrays], core_ids=[0])
    return r.results[0]["out"].reshape(B, T, D)
```
